# Optimizing a Trainium2 kernel written in Bass

```python
import numpy as np
import jax
import jax.numpy as jnp

def _softmax(x, axis=-1):
    return jax.nn.softmax(x, axis=axis)

def _gelu(x):
    return jax.nn.gelu(x, approximate=True)

def _silu(x):
    return jax.nn.silu(x)

def _sigmoid(x):
    return jax.nn.sigmoid(x)

def _layernorm(x, axis=-1, eps=1e-05):
    m = jnp.mean(x, axis=axis, keepdims=True)
    v = jnp.var(x, axis=axis, keepdims=True)
    return (x - m) / jnp.sqrt(v + eps)

def _scatter_add(tgt, idx, src, axis=0):
    return tgt.at[idx].add(src)

def _segment_sum(src, seg, n):
    return jax.ops.segment_sum(src, seg, n)
kernel_name = 'mk_adj_preln_d1_adj_r2_b6136f'

def setup_inputs(seed: int=0):
    np.random.seed(seed)
    _w = jnp.asarray

    def _rec_inputs():
        import jax
        import jax.numpy as jnp
        _gk = jax.random.key(seed)
        x = 0.0002141 + 1 * jax.random.normal(jax.random.fold_in(_gk, 1), (8192, 64), jnp.float32)
        _w = (1.0 + jnp.arange(8192, dtype=jnp.float32)) ** (-0.5)
        _w = _w / _w.mean()
        _pij = jnp.clip(0.000976562 * _w[:, None] * _w[None, :], 0.0, 1.0)
        _a = jax.random.uniform(jax.random.fold_in(_gk, 2), (8192, 8192)) < _pij
        _a = jnp.logical_or(_a, jnp.eye(8192, dtype=bool))
        _af = _a.astype(jnp.float32)
        _af = _af * jax.random.uniform(jax.random.fold_in(_gk, 3), (8192, 8192), jnp.float32, 0.05, 1)
        adj = _af
        return (x, adj)
    x, adj = _rec_inputs()

    def _L0_gnn_setup():
        import jax, jax.numpy as jnp
        import numpy as np
        N, D = (6144, 64)

        def _ggc(x, adj, W, wih, whh, bih, bhh):
            m = adj @ (x @ W)
            gi = m @ wih.T + bih
            gh = x @ whh.T + bhh
            i_r, i_z, i_n = jnp.split(gi, 3, axis=-1)
            h_r, h_z, h_n = jnp.split(gh, 3, axis=-1)
            r = jax.nn.sigmoid(i_r + h_r)
            z = jax.nn.sigmoid(i_z + h_z)
            n = jnp.tanh(i_n + r * h_n)
            return (1.0 - z) * n + z * x
        key = jax.random.key(seed)
        ks = jax.random.split(key, 8)
        s = 1.0 / np.sqrt(D)
        return {'x': jax.random.normal(ks[0], (N, D), jnp.float32), 'adj': jax.random.uniform(ks[1], (N, N), jnp.float32), 'W1': jax.random.normal(ks[2], (D, D), jnp.float32) * s, 'wih1': jax.random.normal(ks[3], (3 * D, D), jnp.float32) * s, 'whh1': jax.random.normal(ks[4], (3 * D, D), jnp.float32) * s, 'bih1': jnp.zeros((3 * D,), jnp.float32), 'bhh1': jnp.zeros((3 * D,), jnp.float32), 'W2': jax.random.normal(ks[5], (D, D), jnp.float32) * s, 'wih2': jax.random.normal(ks[6], (3 * D, D), jnp.float32) * s, 'whh2': jax.random.normal(ks[7], (3 * D, D), jnp.float32) * s, 'bih2': jnp.zeros((3 * D,), jnp.float32), 'bhh2': jnp.zeros((3 * D,), jnp.float32)}
    _L0_gnn_all = _L0_gnn_setup()
    _L0_gnn_in = {k: v for k, v in _L0_gnn_all.items() if k in ('W1', 'wih1', 'whh1', 'bih1', 'bhh1', 'W2', 'wih2', 'whh2', 'bih2', 'bhh2')}
    del _L0_gnn_all
    return {'x': x, 'adj': adj, 'L0_gnn_W1': _L0_gnn_in['W1'], 'L0_gnn_wih1': _L0_gnn_in['wih1'], 'L0_gnn_whh1': _L0_gnn_in['whh1'], 'L0_gnn_bih1': _L0_gnn_in['bih1'], 'L0_gnn_bhh1': _L0_gnn_in['bhh1'], 'L0_gnn_W2': _L0_gnn_in['W2'], 'L0_gnn_wih2': _L0_gnn_in['wih2'], 'L0_gnn_whh2': _L0_gnn_in['whh2'], 'L0_gnn_bih2': _L0_gnn_in['bih2'], 'L0_gnn_bhh2': _L0_gnn_in['bhh2']}

def reference(x, adj, L0_gnn_W1, L0_gnn_wih1, L0_gnn_whh1, L0_gnn_bih1, L0_gnn_bhh1, L0_gnn_W2, L0_gnn_wih2, L0_gnn_whh2, L0_gnn_bih2, L0_gnn_bhh2):
    import jax
    import jax.numpy as jnp

    def _L0_gnn_ref(x, adj, W1, wih1, whh1, bih1, bhh1, W2, wih2, whh2, bih2, bhh2):
        import jax, jax.numpy as jnp
        import numpy as np
        N, D = (6144, 64)

        def _ggc(x, adj, W, wih, whh, bih, bhh):
            m = adj @ (x @ W)
            gi = m @ wih.T + bih
            gh = x @ whh.T + bhh
            i_r, i_z, i_n = jnp.split(gi, 3, axis=-1)
            h_r, h_z, h_n = jnp.split(gh, 3, axis=-1)
            r = jax.nn.sigmoid(i_r + h_r)
            z = jax.nn.sigmoid(i_z + h_z)
            n = jnp.tanh(i_n + r * h_n)
            return (1.0 - z) * n + z * x
        h = jax.nn.relu(_ggc(x, adj, W1, wih1, whh1, bih1, bhh1))
        return jax.nn.relu(_ggc(h, adj, W2, wih2, whh2, bih2, bhh2))
    h = jnp.maximum(_layernorm(x, axis=-1), 0.0)
    x = x + _L0_gnn_ref(h, adj, L0_gnn_W1, L0_gnn_wih1, L0_gnn_whh1, L0_gnn_bih1, L0_gnn_bhh1, L0_gnn_W2, L0_gnn_wih2, L0_gnn_whh2, L0_gnn_bih2, L0_gnn_bhh2)
    return x

_drawn_inputs = setup_inputs


def setup_inputs(seed=0):
    import zlib

    import numpy as np

    out = dict(_drawn_inputs(seed))
    spreads = {'L0_gnn_bih1': (0.0, 0.328),
     'L0_gnn_bhh1': (0.0, 0.573),
     'L0_gnn_bih2': (0.0, 0.33),
     'L0_gnn_bhh2': (0.0, 0.543)}
    factors = {}
    for name, (base, spread) in spreads.items():
        noise = np.random.default_rng([zlib.crc32(name.encode()), seed]).standard_normal(out[name].shape)
        drawn = base * np.exp(spread * noise) if base else spread * noise
        out[name] = jnp.asarray(drawn.astype(out[name].dtype))
    for name, factor in factors.items():
        out[name] = (out[name] * factor).astype(out[name].dtype)
    return out
```

```python
import concourse.bass as bass
from concourse import mybir
from contextlib import ExitStack


def adjacency_gru_two_layers(nc: bass.Bass, adj: bass.AP, x: bass.AP, consts: bass.AP, out: bass.AP):
    fp32, bf16 = mybir.dt.float32, mybir.dt.bfloat16
    ALU, ACT, AX = mybir.AluOpType, mybir.ActivationFunctionType, mybir.AxisListType

    N, D = 8192, 64
    P = 128
    BLK = 512
    NB = N // BLK
    C = BLK // P
    FAR = NB - 2
    RING = FAR // 2
    STAGES = 2
    TILES = NB * NB
    PAIRS = FAR // 2
    Q = 4
    BQ = NB // Q
    EPS = 1e-5
    Y2, Y1 = slice(0, D), slice(D, 2 * D)
    LO, HI = slice(0, D), slice(D, 2 * D)
    WG = [slice(0, 256), slice(256, 512)]
    BIAS = [slice(512, 768), slice(768, 1024)]
    BHH = [slice(1024, 1152), slice(1152, 1280)]
    W = [slice(1280, 1344), slice(1344, 1408)]
    IDENT = slice(1408, 1536)

    ctx = ExitStack()
    with ctx:
        def sb(name, shape, dt=fp32):
            return ctx.enter_context(nc.sbuf_tensor(name, shape, dt))

        def pb(name, shape):
            return ctx.enter_context(nc.psum_tensor(name, shape, fp32))

        def sem(name):
            return ctx.enter_context(nc.semaphore(name))

        cst = sb("cst", [P, 1536])
        eps = sb("eps", [P, 1])
        zeros = sb("zeros", [P, BLK], bf16)
        y = sb("y", [P, NB, C, 2 * D])
        feat = sb("feat", [P, NB, BLK])
        h_tok = sb("h_tok", [P, NB * C, D])
        ring = sb("ring", [P, RING, C, BLK])
        near = sb("near", [P, 2, C, BLK])
        diag = sb("diag", [P, C, BLK])
        stage = sb("stage", [P, STAGES, C, 2 * D])
        cat = sb("cat", [P, BLK])
        m_sum = sb("m_sum", [P, BLK])
        m_up = sb("m_up", [P, BLK])
        m_diag_up = sb("m_diag_up", [P, BLK])
        gates = sb("gates", [P, C, 256])
        rz = sb("rz", [P, C, 2 * D])
        n_pre = sb("n_pre", [P, C, D])
        n_gate = sb("n_gate", [P, C, D])
        h_mix = sb("h_mix", [P, C, D])
        h_new = sb("h_new", [P, C, D])
        hT_new = sb("hT_new", [D, BLK])
        y2_new = sb("y2_new", [P, C, D])
        x_blk = sb("x_blk", [P, C, D])
        ln_stat = sb("ln_stat", [P, Q, 3, BQ * C])
        ln_sq = diag[:, :, :].rearrange("p c (k d) -> p (c k) d", d=D)

        acc_low = pb("acc_low", [P, BLK])
        acc_up = pb("acc_up", [P, BLK])
        acc_a = pb("acc_a", [P, BLK])
        acc_b = pb("acc_b", [P, BLK])
        g_ps = pb("g_ps", [P, C, 256])
        t_ps = pb("t_ps", [P, BLK])
        y_ps = pb("y_ps", [P, C, D])

        consts_in = sem("consts_in")
        x_in = [sem(f"x_in{k}") for k in range(Q)]
        zeros_set = sem("zeros_set")
        eps_set = sem("eps_set")
        x_squared = sem("x_squared")
        x_centred = sem("x_centred")
        squares_summed = sem("squares_summed")
        std_ready = sem("std_ready")
        h0_ready = sem("h0_ready")
        h0_transposed = sem("h0_transposed")
        h0T_copied = sem("h0T_copied")
        y1_multiplied = sem("y1_multiplied")
        y1_copied = sem("y1_copied")
        ring_in = [sem(f"ring_in{k}") for k in range(RING)]
        near_in = sem("near_in")
        diag_in = sem("diag_in")
        stage_ready = sem("stage_ready")
        tile_done = sem("tile_done")
        up_read = sem("up_read")
        low_read = sem("low_read")
        up_moved = sem("up_moved")
        low_moved = sem("low_moved")
        diag_moved = sem("diag_moved")
        cat_h = sem("cat_h")
        cat_m = sem("cat_m")
        gates_done = sem("gates_done")
        gates_ready = sem("gates_ready")
        rz_ready = sem("rz_ready")
        n_pre_ready = sem("n_pre_ready")
        n_ready = sem("n_ready")
        h_new_ready = sem("h_new_ready")
        hT_done = sem("hT_done")
        hT_ready = sem("hT_ready")
        h_kept = sem("h_kept")
        y2_done = sem("y2_done")
        y2_new_ready = sem("y2_new_ready")
        y2_ready = sem("y2_ready")
        diag_m2_done = sem("diag_m2_done")
        near_m2_done = sem("near_m2_done")
        diag_m2_moved = sem("diag_m2_moved")
        near_m2_moved = sem("near_m2_moved")
        held_read = sem("held_read")
        x_blk_in = sem("x_blk_in")
        out_ready = sem("out_ready")
        out_written = sem("out_written")
        dve_step = sem("dve_step")
        sp_passed = sem("sp_passed")
        pool_passed = sem("pool_passed")
        dve_passed = sem("dve_passed")

        from_one = {"pool": [h_kept], "pe": [gates_done], "dve": [up_read, low_read, held_read, y2_ready]}

        block = ctx.enter_context(nc.Block())

        def within(v, low, high):
            if isinstance(v, int):
                return v
            return nc.s_assert_within(v, low, high, skip_runtime_bounds_check_because="the branch taken bounds it")

        @block.sync
        def _(sp):
            sp.dma_start(h_tok[:, 0:BQ * C, :], x[:, 0:BQ * C, :]).then_inc(x_in[0], 16)
            sp.dma_start(cst[:, :], consts).then_inc(consts_in, 16)
            for k in range(1, Q):
                part = slice(k * BQ * C, (k + 1) * BQ * C)
                sp.dma_start(h_tok[:, part, :], x[:, part, :]).then_inc(x_in[k], 16)
            for q in range(RING):
                sp.dma_start(ring[:, q], adj[0, q]).then_inc(ring_in[q], 16)
            with sp.Fori(0, NB) as t:
                for q in range(FAR):
                    if q == RING:
                        slot = sp.snap(t & 1)
                        sp.wait_ge(held_read, t + 1)
                        sp.sem_inc(sp_passed, 1)
                        sp.dma_start(near[:, slot], adj[t, NB - 1]).then_inc(near_in, 16)
                        sp.dma_start(diag[:, :, :], adj[t, NB - 2]).then_inc(diag_in, 16)
                    done = sp.snap(NB * t + q + 1)
                    if q < RING:
                        sp.wait_ge(tile_done, done)
                        sp.sem_inc(sp_passed, 1)
                        sp.dma_start(ring[:, q], adj[t, q + RING]).then_inc(ring_in[q], 16)
                    else:
                        with sp.If(t < NB - 1):
                            row = sp.snap(within(t + 1, 1, NB - 1))
                            sp.wait_ge(tile_done, done)
                            sp.sem_inc(sp_passed, 1)
                            sp.dma_start(ring[:, q - RING], adj[row, q - RING]).then_inc(ring_in[q - RING], 16)
                        with sp.Else():
                            sp.wait_ge(tile_done, done)
                            sp.sem_inc(sp_passed, 1)
                            sp.dma_start(ring[:, q - RING], adj[0, q - RING]).then_inc(ring_in[q - RING], 16)

            def load_again(j, q, done, least=0):
                s = q % RING
                row_a = sp.snap(within(FAR - j, 0, NB - 1))
                if least > q:
                    sp.wait_ge(tile_done, done)
                    sp.sem_inc(sp_passed, 1)
                    sp.dma_start(ring[:, s], adj[row_a, q]).then_inc(ring_in[s], 16)
                    return

                def row_b():
                    row = sp.snap(within(j, 0, q))
                    col = sp.snap(within(q - j, 0, q))
                    sp.wait_ge(tile_done, done)
                    sp.sem_inc(sp_passed, 1)
                    sp.dma_start(ring[:, s], adj[row, col]).then_inc(ring_in[s], 16)

                if q >= PAIRS - 1:
                    row_b()
                    return
                with sp.If(j > q):
                    sp.wait_ge(tile_done, done)
                    sp.sem_inc(sp_passed, 1)
                    sp.dma_start(ring[:, s], adj[row_a, q]).then_inc(ring_in[s], 16)
                with sp.Else():
                    row_b()

            with sp.Fori(0, PAIRS) as j:
                for q in range(FAR):
                    done = sp.snap(TILES + FAR * j + q + 1)
                    if q < RING:
                        load_again(j, q + RING, done)
                    else:
                        with sp.If(j < PAIRS - 1):
                            load_again(within(j + 1, 1, PAIRS - 1), q - RING, done, 1)
                        with sp.Else():
                            sp.wait_ge(tile_done, done)
                            sp.sem_inc(sp_passed, 1)
                            sp.dma_start(ring[:, q - RING], adj[PAIRS, q - RING]).then_inc(ring_in[q - RING], 16)

        @block.gpsimd
        def _(pool):
            def stage_first(s, t, need):
                b = s % STAGES
                if s == NB - 2:
                    g, split = t + 1, NB - 1
                elif s == NB - 1:
                    g, split = t, None
                else:
                    g, split = t + 2 + s, NB - 2 - s
                if split is None or isinstance(t, int):
                    g = g if isinstance(g, int) else pool.snap(g)
                    need()
                    pool.tensor_copy(stage[:, b, :, Y1], y[:, g, :, Y1]).then_inc(stage_ready, 1)
                    return
                with pool.If(t < split):
                    gu = pool.snap(within(g, 0, NB - 1))
                    need()
                    pool.tensor_copy(stage[:, b, :, Y1], y[:, gu, :, Y1]).then_inc(stage_ready, 1)
                with pool.Else():
                    gl = pool.snap(within(g - NB, 0, NB - 1))
                    need()
                    pool.tensor_copy(stage[:, b, :, :], y[:, gl, :, :]).then_inc(stage_ready, 1)

            def stage_again(s, j, need, least=0):
                b = s % STAGES
                if least > s:
                    ga = pool.snap(within(NB - j + s, 0, NB - 1))
                    need()
                    pool.tensor_copy(stage[:, b, :, Y2], y[:, ga, :, Y2]).then_inc(stage_ready, 1)
                    return
                if s >= PAIRS - 1:
                    need()
                    pool.tensor_copy(stage[:, b, :, Y2], y[:, s + 2, :, Y2]).then_inc(stage_ready, 1)
                    return
                with pool.If(j > s):
                    ga = pool.snap(within(NB - j + s, 0, NB - 1))
                    need()
                    pool.tensor_copy(stage[:, b, :, Y2], y[:, ga, :, Y2]).then_inc(stage_ready, 1)
                with pool.Else():
                    need()
                    pool.tensor_copy(stage[:, b, :, Y2], y[:, s + 2, :, Y2]).then_inc(stage_ready, 1)

            def keep_h(row, count):
                at = pool.snap(row * C) if not isinstance(row, int) else row * C
                pool.wait_ge(hT_ready, count)
                pool.sem_inc(pool_passed, 1)
                pool.tensor_copy(feat[LO, row], hT_new[:, :])
                pool.tensor_copy(h_tok[:, bass.ds(at, C), :], h_new[:, :, :]).then_inc(h_kept, 1)

            def cat_hidden(row, count):
                pool.wait_ge(gates_done, count + 1)
                pool.sem_inc(pool_passed, 1)
                pool.tensor_copy(cat[LO, :], feat[LO, row]).then_inc(cat_h, 1)

            for s in from_one["pool"]:
                pool.sem_inc(s, 1)
            pool.memset(eps[:, :], EPS).then_inc(eps_set, 1)
            pool.memset(zeros[:, :], 0.0).then_inc(zeros_set, 1)
            pool.wait_ge(y1_copied, NB)
            for s in range(STAGES):
                stage_first(s, 0, lambda: None)
            with pool.Fori(0, NB) as t:
                for s in range(NB):
                    n = s + STAGES
                    done = pool.snap(NB * t + s + 1)

                    def need():
                        pool.wait_ge(tile_done, done)
                        pool.sem_inc(pool_passed, 1)

                    if n == FAR - 1:
                        pool.wait_ge(y2_ready, t + 1)
                        pool.sem_inc(pool_passed, 1)
                    if n < NB:
                        stage_first(n, t, need)
                    else:
                        with pool.If(t < NB - 1):
                            stage_first(n - NB, within(t + 1, 1, NB - 1), need)
                    if s == FAR - 4:
                        with pool.If(t >= 1):
                            keep_h(pool.snap(within(t - 1, 0, NB - 2)), t)
                    if s == FAR - 2:
                        cat_hidden(t, t)
            keep_h(NB - 1, NB)
            pool.wait_ge(h_kept, NB + 1)
            cat_hidden(NB - 1, NB)
            pool.wait_ge(tile_done, TILES)
            for s in range(STAGES):
                pool.tensor_copy(stage[:, s, :, Y2], y[:, s + 2, :, Y2]).then_inc(stage_ready, 1)
            with pool.Fori(0, PAIRS) as j:
                for s in range(FAR):
                    n = s + STAGES
                    done = pool.snap(TILES + FAR * j + s + 1)

                    def need():
                        pool.wait_ge(tile_done, done)
                        pool.sem_inc(pool_passed, 1)

                    if n < FAR:
                        if n == FAR - 1:
                            pool.wait_ge(y2_ready, NB + 1)
                        stage_again(n, j, need)
                    else:
                        with pool.If(j < PAIRS - 1):
                            stage_again(n - FAR, within(j + 1, 1, PAIRS - 1), need, 1)
                        with pool.Else():
                            need()
                            pool.tensor_copy(stage[:, n - FAR, :, Y2], y[:, PAIRS + 2 + n - FAR, :, Y2])\
                                .then_inc(stage_ready, 1)
                    if s == 2:
                        with pool.If(j >= 1):
                            cat_hidden(pool.snap(within(j - 1, 0, PAIRS - 1)), NB + 2 * j)
                    if s == 9:
                        cat_hidden(pool.snap(within(FAR - j, PAIRS, FAR)), NB + 1 + 2 * j)
            first = TILES + FAR * PAIRS
            for s in range(STAGES, PAIRS):
                pool.wait_ge(tile_done, first + s - STAGES + 1)
                pool.tensor_copy(stage[:, s % STAGES, :, Y2], y[:, PAIRS + 2 + s, :, Y2]).then_inc(stage_ready, 1)
                if s == 4:
                    cat_hidden(PAIRS - 1, NB + 2 * PAIRS)
            cat_hidden(PAIRS, NB + 1 + 2 * PAIRS)

        @block.tensor
        def _(pe):
            def halves(acc, st, cols, tile, first=False):
                for c in range(C):
                    half = (LO, HI)[c % 2]
                    last = pe.matmul(acc[half, :], st[:, c, cols], tile[:, c, :], start=first and c < 2, stop=True,
                                     skip_group_check=True)
                return last

            def full(acc, st, tile):
                for c in range(C):
                    last = pe.matmul(acc[:, :], st[:, c, :], tile[:, c, :], start=False, stop=True,
                                     skip_group_check=True)
                return last

            def clear(acc):
                pe.matmul(acc[:, :], zeros[:, 0:P], zeros[:, :], start=True, stop=True)

            def gate_products(layer, count):
                pe.wait_ge(cat_h, count)
                pe.wait_ge(cat_m, count)
                for c in range(C):
                    last = pe.matmul(g_ps[:, c, :], cat[:, c * P:(c + 1) * P], cst[:, WG[layer]], start=True,
                                     stop=True)
                last.then_inc(gates_done, 1)

            def transpose_h(count):
                pe.wait_ge(h_new_ready, count)
                for c in range(C):
                    last = pe.matmul(t_ps[LO, c * P:(c + 1) * P], h_new[:, c, :], cst[:, IDENT], start=True, stop=True)
                last.then_inc(hT_done, 1)

            def new_y2(count):
                pe.wait_ge(hT_ready, count)
                for c in range(C):
                    last = pe.matmul(y_ps[:, c, :], hT_new[:, c * P:(c + 1) * P], cst[LO, W[1]], start=True,
                                     stop=True)
                last.then_inc(y2_done, 1)

            def held_diag(count):
                pe.wait_ge(y2_new_ready, count)
                halves(acc_b, y2_new, slice(0, D), diag, first=True).then_inc(diag_m2_done, 1)

            def held_near(parity):
                halves(acc_a, y2_new, slice(0, D), near[:, parity], first=True).then_inc(near_m2_done, 1)

            for s in from_one["pe"]:
                pe.sem_inc(s, 1)
            pe.wait_ge(consts_in, 16)
            t_banks, y_banks = (t_ps, acc_low), (y_ps, acc_up[:, 0:C * D].rearrange("p (c d) -> p c d", d=D))

            def transpose_h0(b):
                pe.wait_ge(h0_ready, b // BQ + 1)
                for c in range(C):
                    last = pe.matmul(t_banks[b % 2][LO, c * P:(c + 1) * P], h_tok[:, b * C + c, :], cst[:, IDENT], start=True, stop=True)
                last.then_inc(h0_transposed, 1)

            transpose_h0(0)
            for b in range(NB):
                if b + 1 < NB:
                    if b >= 1:
                        pe.wait_ge(h0T_copied, b)
                    transpose_h0(b + 1)
                pe.wait_ge(h0T_copied, b + 1)
                if b >= 2:
                    pe.wait_ge(y1_copied, b - 1)
                for c in range(C):
                    last = pe.matmul(y_banks[b % 2][:, c, :], feat[LO, b, c * P:(c + 1) * P], cst[LO, W[0]],
                                     start=True, stop=True)
                last.then_inc(y1_multiplied, 1)
            pe.wait_ge(zeros_set, 1)
            pe.wait_ge(y1_copied, NB)

            def held_work(q, t, parity, layer_count):
                if q == 0:
                    gate_products(0, layer_count)
                elif q == 4:
                    transpose_h(layer_count)
                elif q == 5:
                    new_y2(layer_count)
                elif q == 6:
                    held_diag(layer_count)

            with pe.Fori(0, NB // 2) as u:
                for parity in range(2):
                    t = pe.snap(2 * u + parity)
                    pe.wait_ge(up_read, t + 1)
                    clear(acc_up)
                    pe.wait_ge(low_read, t + 1)
                    clear(acc_low)
                    for q in range(FAR):
                        s, slot = q % STAGES, ring[:, q % RING]
                        pe.wait_ge(stage_ready, NB * t + q + 1)
                        pe.wait_ge(ring_in[q % RING], 32 * t + 16 * (q // RING + 1))
                        with pe.If(t < NB - 2 - q):
                            halves(acc_up, stage[:, s], Y1, slot).then_inc(tile_done, 1)
                        with pe.Else():
                            full(acc_low, stage[:, s], slot).then_inc(tile_done, 1)
                        if q in (0, 4, 5, 6):
                            if parity:
                                held_work(q, t, parity, t)
                            else:
                                with pe.If(u >= 1):
                                    held_work(q, t, parity, t)
                        if q == 6:
                            with pe.If(u >= 1):
                                held_near(parity)
                    pe.wait_ge(stage_ready, NB * t + NB - 1)
                    pe.wait_ge(near_in, 16 * t + 16)
                    with pe.If(t < NB - 1):
                        halves(acc_up, stage[:, 0], Y1, near[:, parity]).then_inc(tile_done, 1)
                    with pe.Else():
                        full(acc_low, stage[:, 0], near[:, parity]).then_inc(tile_done, 1)
                    pe.wait_ge(stage_ready, NB * t + NB)
                    pe.wait_ge(diag_in, 16 * t + 16)
                    pe.wait_ge(held_read, t + 1)
                    halves(acc_a, stage[:, 1], Y1, diag, first=True).then_inc(tile_done, 1)
            for q in (0, 4, 5, 6):
                held_work(q, NB, 0, NB)
            held_near(0)

            def row_products(q, n_items, uses):
                pe.wait_ge(stage_ready, n_items)
                pe.wait_ge(ring_in[q % RING], uses)

            gate_products(1, NB + 1)
            with pe.Fori(0, PAIRS) as j:
                for acc, free in ((acc_up, up_read), (acc_low, low_read)):
                    pe.wait_ge(free, NB + j + 1)
                    clear(acc)
                for q in range(FAR):
                    row_products(q, TILES + FAR * j + q + 1, 32 * NB + 32 * j + 16 * (q // RING + 1))
                    if q >= PAIRS - 1:
                        halves(acc_up, stage[:, q % STAGES], Y2, ring[:, q % RING]).then_inc(tile_done, 1)
                    else:
                        with pe.If(j > q):
                            halves(acc_low, stage[:, q % STAGES], Y2, ring[:, q % RING]).then_inc(tile_done, 1)
                        with pe.Else():
                            halves(acc_up, stage[:, q % STAGES], Y2, ring[:, q % RING]).then_inc(tile_done, 1)
                    if q == 0:
                        with pe.If(j >= 1):
                            gate_products(1, NB + 2 * j)
                    if q == 6:
                        with pe.If(j >= 1):
                            gate_products(1, NB + 1 + 2 * j)
            pe.wait_ge(up_read, NB + PAIRS + 1)
            clear(acc_up)
            for q in range(PAIRS):
                row_products(q, TILES + FAR * PAIRS + q + 1, 32 * NB + 32 * PAIRS + 16)
                halves(acc_up, stage[:, q % STAGES], Y2, ring[:, q % RING]).then_inc(tile_done, 1)
                if q == 0:
                    gate_products(1, NB + 2 * PAIRS)
                if q == 4:
                    gate_products(1, NB + 1 + 2 * PAIRS)
            gate_products(1, NB + 2 + 2 * PAIRS)

        @block.scalar
        def _(act):
            def copy_h0T(b):
                act.wait_ge(h0_transposed, b + 1)
                act.activation(feat[LO, b], (t_ps, acc_low)[b % 2][LO, :], ACT.Copy).then_inc(h0T_copied, 1)

            def copy_y1(b):
                act.wait_ge(y1_multiplied, b + 1)
                src = y_ps if b % 2 == 0 else acc_up[:, 0:C * D].rearrange("p (c d) -> p c d", d=D)
                act.activation(y[:, b, :, Y1], src[:, :, :], ACT.Copy).then_inc(y1_copied, 1)

            act.wait_ge(eps_set, 1)
            for k in range(Q):
                part = slice(k * BQ * C, (k + 1) * BQ * C)
                act.wait_ge(x_centred, k + 1)
                act.activation(ln_sq[:, (k % 2) * BQ * C:(k % 2 + 1) * BQ * C, :], h_tok[:, part, :],
                               ACT.Square).then_inc(x_squared, 1)
                act.wait_ge(squares_summed, k + 1)
                act.activation(ln_stat[:, k, 2, :], ln_stat[:, k, 2, :], ACT.Sqrt, bias=eps[:, :], scale=1.0 / D)\
                    .then_inc(std_ready, 1)
                if k >= 1:
                    for b in range((k - 1) * BQ, k * BQ):
                        copy_h0T(b)
                        copy_y1(b)
            for b in range((Q - 1) * BQ, NB):
                copy_h0T(b)
                copy_y1(b)

            def gate_functions(count):
                act.wait_ge(gates_ready, count)
                act.activation(rz[:, :, :], gates[:, :, 0:2 * D], ACT.Sigmoid).then_inc(rz_ready, 1)
                act.wait_ge(n_pre_ready, count)
                act.activation(n_gate[:, :, :], n_pre[:, :, :], ACT.Tanh).then_inc(n_ready, 1)

            with act.Fori(0, NB) as t:
                act.wait_ge(tile_done, NB * t + NB - 1)
                act.activation(m_up[HI, :], acc_up[LO, :], ACT.Copy).then_inc(up_moved, 1)
                act.activation(feat[HI, t], acc_low[LO, :], ACT.Copy).then_inc(low_moved, 1)
                act.wait_ge(tile_done, NB * t + NB)
                act.activation(m_diag_up[HI, :], acc_a[LO, :], ACT.Copy).then_inc(diag_moved, 1)
                gate_functions(t + 1)
                act.wait_ge(h_kept, t + 1)
                act.wait_ge(hT_done, t + 1)
                act.activation(hT_new[:, :], t_ps[LO, :], ACT.Copy).then_inc(hT_ready, 1)
                act.wait_ge(diag_m2_done, t + 1)
                act.activation(m_up[HI, :], acc_b[LO, :], ACT.Copy).then_inc(diag_m2_moved, 1)
                with act.If(t >= 1):
                    act.wait_ge(near_m2_done, t)
                    act.activation(m_diag_up[HI, :], acc_a[LO, :], ACT.Copy).then_inc(near_m2_moved, 1)

            def finish_row(row, count, order):
                at = row * C if isinstance(row, int) else act.snap(row * C)
                act.dma_start(x_blk[:, :, :], x[:, bass.ds(at, C), :]).then_inc(x_blk_in, 16)
                gate_functions(count)
                act.wait_ge(out_ready, order + 1)
                act.dma_start(out[:, bass.ds(at, C), :], h_new[:, :, :]).then_inc(out_written, 16)

            finish_row(NB - 1, NB + 1, 0)
            with act.Fori(0, PAIRS) as j:
                act.wait_ge(tile_done, TILES + FAR * j + FAR)
                act.activation(m_up[HI, :], acc_low[LO, :], ACT.Copy).then_inc(low_moved, 1)
                act.activation(m_diag_up[HI, :], acc_up[LO, :], ACT.Copy).then_inc(up_moved, 1)
                finish_row(act.snap(within(FAR - j, PAIRS, FAR)), NB + 2 + 2 * j, 2 * j + 1)
                finish_row(j, NB + 3 + 2 * j, 2 * j + 2)
            act.wait_ge(tile_done, TILES + FAR * PAIRS + PAIRS)
            act.activation(m_diag_up[HI, :], acc_up[LO, :], ACT.Copy).then_inc(up_moved, 1)
            finish_row(PAIRS, NB + 2 + 2 * PAIRS, 2 * PAIRS + 1)
            act.wait_ge(out_written, 16 * NB)

        @block.vector
        def _(dve):
            class Chain:
                n = 0

            def step(ins):
                Chain.n += 1
                ins.then_inc(dve_step, 1)
                dve.wait_ge(dve_step, Chain.n)

            def new_chain():
                Chain.n = 0
                dve.sem_clear(dve_step)

            for s in from_one["dve"]:
                dve.sem_inc(s, 1)
            for k in range(Q):
                part = h_tok[:, k * BQ * C:(k + 1) * BQ * C, :]
                mean, rstd, var = (ln_stat[:, k, r, :] for r in range(3))
                dve.wait_ge(x_in[k], 16)
                step(dve.tensor_reduce(mean, part, AX.X, ALU.add))
                step(dve.tensor_scalar(mean, mean, 1.0 / D, None, ALU.mult))
                dve.tensor_tensor(part, part, mean.unsqueeze(2).to_broadcast([P, BQ * C, D]), ALU.subtract)\
                    .then_inc(x_centred, 1)
                dve.wait_ge(x_squared, k + 1)
                dve.tensor_reduce(var, ln_sq[:, (k % 2) * BQ * C:(k % 2 + 1) * BQ * C, :], AX.X, ALU.add)\
                    .then_inc(squares_summed, 1)
                dve.wait_ge(std_ready, k + 1)
                step(dve.reciprocal(rstd, var))
                dve.scalar_tensor_tensor(out=part, in0=part, scalar=0.0,
                                         in1=rstd.unsqueeze(2).to_broadcast([P, BQ * C, D]),
                                         op0=ALU.max, op1=ALU.mult).then_inc(h0_ready, 1)
            dve.wait_ge(consts_in, 16)
            for layer in range(2):
                rz_bias = cst[:, BIAS[layer].start:BIAS[layer].start + 2 * D]
                step(dve.tensor_tensor(rz_bias, rz_bias, cst[:, BHH[layer]], ALU.add))

            def new_state(layer, row, count):
                at = row * C if isinstance(row, int) else dve.snap(row * C)
                h = h_tok[:, bass.ds(at, C), :]
                dve.wait_ge(gates_done, count + 1)
                dve.tensor_tensor(gates[:, :, :], g_ps[:, :, :],
                                  cst[:, BIAS[layer]].unsqueeze(1).to_broadcast([P, C, 256]), ALU.add)\
                    .then_inc(gates_ready, 1)
                dve.wait_ge(rz_ready, count)
                step(dve.tensor_tensor(n_pre[:, :, :], rz[:, :, 0:D], gates[:, :, 3 * D:4 * D], ALU.mult))
                dve.tensor_tensor(n_pre[:, :, :], n_pre[:, :, :], gates[:, :, 2 * D:3 * D], ALU.add)\
                    .then_inc(n_pre_ready, 1)
                dve.wait_ge(n_ready, count)
                step(dve.tensor_tensor(h_mix[:, :, :], h, n_gate[:, :, :], ALU.subtract))
                step(dve.tensor_tensor(h_mix[:, :, :], h_mix[:, :, :], rz[:, :, D:2 * D], ALU.mult))
                step(dve.tensor_tensor(h_mix[:, :, :], h_mix[:, :, :], n_gate[:, :, :], ALU.add))

            def add_held(acc, up, moved, count, row):
                dve.wait_ge(moved, count)
                step(dve.tensor_tensor(m_sum[HI, :], acc[HI, :], up[HI, :], ALU.add))
                return dve.tensor_tensor(feat[HI, row], m_sum[HI, :], feat[HI, row], ALU.add)

            with dve.Fori(0, NB) as t:
                new_chain()
                dve.wait_ge(up_moved, t + 1)
                ins = dve.tensor_tensor(m_sum[HI, :], acc_up[HI, :], m_up[HI, :], ALU.add)
                ins.then_inc(up_read, 1)
                dve.wait_ge(up_read, t + 2)
                dve.wait_ge(low_moved, t + 1)
                ins = dve.tensor_tensor(m_sum[HI, :], acc_low[HI, :], m_sum[HI, :], ALU.add)
                ins.then_inc(low_read, 1)
                dve.wait_ge(low_read, t + 2)
                dve.wait_ge(diag_moved, t + 1)
                step(dve.tensor_tensor(m_sum[HI, :], acc_a[HI, :], m_sum[HI, :], ALU.add))
                dve.wait_ge(gates_done, t + 1)
                dve.tensor_tensor(cat[HI, :], m_sum[HI, :], m_diag_up[HI, :], ALU.add).then_inc(cat_m, 1)
                new_state(0, t, t + 1)
                dve.wait_ge(h_kept, t + 1)
                dve.tensor_scalar(h_new[:, :, :], h_mix[:, :, :], 0.0, None, ALU.max).then_inc(h_new_ready, 1)
                dve.wait_ge(y2_done, t + 1)
                dve.tensor_copy(y2_new[:, :, :], y_ps[:, :, :]).then_inc(y2_new_ready, 1)
                dve.tensor_copy(y[:, t, :, Y2], y_ps[:, :, :]).then_inc(y2_ready, 1)
                step(add_held(acc_b, m_up, diag_m2_moved, t + 1, t))
                with dve.If(t >= 1):
                    add_held(acc_a, m_diag_up, near_m2_moved, t, dve.snap(within(t - 1, 0, NB - 2)))\
                        .then_inc(held_read, 1)
                with dve.Else():
                    dve.sem_inc(held_read, 1)
                dve.wait_ge(held_read, t + 2)

            def finish_row(row, count, order):
                dve.wait_ge(cat_m, count)
                new_state(1, row, count)
                if not (isinstance(order, int) and order == 0):
                    dve.wait_ge(out_written, 16 * order)
                dve.wait_ge(x_blk_in, 16 * order + 16)
                ins = dve.scalar_tensor_tensor(out=h_new[:, :, :], in0=h_mix[:, :, :], scalar=0.0,
                                               in1=x_blk[:, :, :], op0=ALU.max, op1=ALU.add)
                ins.then_inc(out_ready, 1)

            new_chain()
            dve.tensor_copy(cat[HI, :], feat[HI, NB - 1]).then_inc(cat_m, 1)
            finish_row(NB - 1, NB + 1, 0)
            with dve.Fori(0, PAIRS) as j:
                new_chain()
                row_a = dve.snap(within(FAR - j, PAIRS, FAR))
                dve.wait_ge(low_moved, NB + 1 + j)
                dve.tensor_tensor(m_sum[HI, :], acc_low[HI, :], m_up[HI, :], ALU.add).then_inc(low_read, 1)
                dve.wait_ge(low_read, NB + 2 + j)
                dve.sem_inc(dve_passed, 1)
                dve.tensor_tensor(cat[HI, :], m_sum[HI, :], feat[HI, row_a], ALU.add).then_inc(cat_m, 1)
                dve.wait_ge(cat_m, NB + 2 + 2 * j)
                dve.wait_ge(up_moved, NB + 1 + j)
                dve.tensor_tensor(m_sum[HI, :], acc_up[HI, :], m_diag_up[HI, :], ALU.add).then_inc(up_read, 1)
                dve.wait_ge(up_read, NB + 2 + j)
                finish_row(row_a, NB + 2 + 2 * j, 2 * j + 1)
                dve.tensor_tensor(cat[HI, :], m_sum[HI, :], feat[HI, j], ALU.add).then_inc(cat_m, 1)
                finish_row(j, NB + 3 + 2 * j, 2 * j + 2)
            new_chain()
            dve.wait_ge(up_moved, NB + 1 + PAIRS)
            step(dve.tensor_tensor(m_sum[HI, :], acc_up[HI, :], m_diag_up[HI, :], ALU.add))
            dve.tensor_tensor(cat[HI, :], m_sum[HI, :], feat[HI, PAIRS], ALU.add).then_inc(cat_m, 1)
            finish_row(PAIRS, NB + 2 + 2 * PAIRS, 2 * PAIRS + 1)


def kernel(**inputs):
    import numpy as np
    import concourse.bacc as bacc
    from concourse.bass_utils import run_bass_kernel_spmd

    N, D, P, BLK = 8192, 64, 128, 512
    NB, C = N // BLK, BLK // P
    a = {k: np.asarray(v) for k, v in inputs.items()}

    adj = a["adj"].reshape(NB, BLK, NB, C, P)
    adj_tiles = np.empty((NB, NB, P, C, BLK), adj.dtype)
    for i in range(NB):
        order = [(i + 2 + s) % NB for s in range(NB)]
        adj_tiles[i] = adj[i][:, order].transpose(1, 3, 2, 0)
    x_tok = np.ascontiguousarray(a["x"].reshape(NB * C, P, D).transpose(1, 0, 2))

    consts = np.zeros((P, 1536), np.float32)
    for layer in range(2):
        name = "L0_gnn_%s" + str(layer + 1)
        whh, wih = a[name % "whh"].T, a[name % "wih"].T
        at = 256 * layer
        consts[0:D, at:at + 2 * D] = whh[:, 0:2 * D]
        consts[D:P, at:at + 2 * D] = wih[:, 0:2 * D]
        consts[D:P, at + 2 * D:at + 3 * D] = wih[:, 2 * D:]
        consts[0:D, at + 3 * D:at + 4 * D] = whh[:, 2 * D:]
        at = 512 + 256 * layer
        consts[:, at:at + 3 * D] = a[name % "bih"]
        consts[:, at + 3 * D:at + 4 * D] = a[name % "bhh"][2 * D:]
        consts[:, 1024 + 128 * layer:1024 + 128 * (layer + 1)] = a[name % "bhh"][0:2 * D]
        consts[0:D, 1280 + D * layer:1280 + D * (layer + 1)] = a[name % "W"]
    consts[:, 1408:1536] = np.eye(P, dtype=np.float32)

    nc = bacc.Bacc("TRN2", target_bir_lowering=False, num_devices=1)
    arrays = {"adj_tiles": adj_tiles, "x_tok": x_tok, "consts": consts}
    args = [nc.dram_tensor(k, v.shape, mybir.dt.from_np(v.dtype), kind="ExternalInput").ap() for k, v in arrays.items()]
    args.append(nc.dram_tensor("out_tok", (P, NB * C, D), mybir.dt.float32, kind="ExternalOutput").ap())
    adjacency_gru_two_layers(nc, *args)
    got = run_bass_kernel_spmd(nc, [arrays], core_ids=[0]).results[0]["out_tok"]
    return np.ascontiguousarray(got.transpose(1, 0, 2)).reshape(N, D)
```

```python
import concourse.bass as bass
from concourse import mybir
from contextlib import ExitStack


def adjacency_gru_two_layers(nc: bass.Bass, adj: bass.AP, x: bass.AP, consts: bass.AP, out: bass.AP):
    fp32, bf16 = mybir.dt.float32, mybir.dt.bfloat16
    ALU, ACT, AX = mybir.AluOpType, mybir.ActivationFunctionType, mybir.AxisListType

    N, D = 8192, 64
    P = 128
    BLK = 512
    NB = N // BLK
    C = BLK // P
    FAR = NB - 2
    RING = FAR // 2
    STAGES = 2
    TILES = NB * NB
    EARLY = RING
    LAG = EARLY + 2
    PAIRS = FAR // 2
    PIECES = [(0, 1), (1, 4), (4, 8), (8, 12), (12, 16)]
    EPS = 1e-5
    Y2, Y1 = slice(0, D), slice(D, 2 * D)
    LO, HI = slice(0, D), slice(D, 2 * D)
    WG = [slice(0, 256), slice(256, 512)]
    BIAS = [slice(512, 768), slice(768, 1024)]
    BHH = [slice(1024, 1152), slice(1152, 1280)]
    W = [slice(1280, 1344), slice(1344, 1408)]
    IDENT = slice(1408, 1536)

    ctx = ExitStack()
    with ctx:
        def sb(name, shape, dt=fp32):
            return ctx.enter_context(nc.sbuf_tensor(name, shape, dt))

        def pb(name, shape):
            return ctx.enter_context(nc.psum_tensor(name, shape, fp32))

        def sem(name):
            return ctx.enter_context(nc.semaphore(name))

        cst = sb("cst", [P, 1536])
        eps = sb("eps", [P, 1])
        zeros = sb("zeros", [P, BLK], bf16)
        y = sb("y", [P, NB, C, 2 * D])
        feat = sb("feat", [P, NB, BLK])
        h_tok = sb("h_tok", [P, NB * C, D])
        ring = sb("ring", [P, RING, C, BLK])
        near = sb("near", [P, 2, C, BLK])
        diag = sb("diag", [P, C, BLK])
        stage = sb("stage", [P, STAGES, C, 2 * D])
        early_stage = sb("early_stage", [P, STAGES, C, D])
        m_early_up = sb("m_early_up", [P, BLK])
        cat = sb("cat", [P, BLK])
        m_sum = sb("m_sum", [P, BLK])
        m_up = sb("m_up", [P, BLK])
        m_diag_up = sb("m_diag_up", [P, BLK])
        gates = sb("gates", [P, C, 256])
        rz = sb("rz", [P, C, 2 * D])
        n_pre = sb("n_pre", [P, C, D])
        n_gate = sb("n_gate", [P, C, D])
        h_mix = sb("h_mix", [P, C, D])
        h_new = sb("h_new", [P, C, D])
        hT_pair = sb("hT_pair", [P, 2, C // 2, P])
        y2_new = sb("y2_new", [P, C, D])
        x_blk = sb("x_blk", [P, C, D])
        ln_stat = sb("ln_stat", [P, 3, NB * C])
        ln_sq = [buf.rearrange("p c (k d) -> p (c k) d", d=D) for buf in (diag[:, :, :], near[:, 1])]

        acc_low = pb("acc_low", [P, BLK])
        acc_up = pb("acc_up", [P, BLK])
        acc_a = pb("acc_a", [P, BLK])
        acc_b = pb("acc_b", [P, BLK])
        g_ps = pb("g_ps", [P, C, 256])
        acc_early = g_ps[:, 0:2, :].rearrange("p c n -> p (c n)")
        t_ps = pb("t_ps", [P, BLK])
        y_ps = pb("y_ps", [P, BLK])

        def t_part(bank):
            return bank[:, 0:2 * P].rearrange("p (k n) -> p k n", n=P)

        def y_parts(t_bank, y_bank):
            return (y_bank[:, 0:2 * D].rearrange("p (k d) -> p k d", d=D),
                    t_bank[:, 2 * P:2 * P + 2 * D].rearrange("p (k d) -> p k d", d=D))

        t_banks, y_banks = (t_ps, acc_low, acc_a), (y_ps, acc_up, acc_b)

        consts_in = sem("consts_in")
        x_in = [sem(f"x_in{k}") for k in range(len(PIECES))]
        zeros_set = sem("zeros_set")
        eps_set = sem("eps_set")
        x_squared = sem("x_squared")
        x_centred = sem("x_centred")
        squares_summed = sem("squares_summed")
        std_ready = sem("std_ready")
        h0_ready = sem("h0_ready")
        h0_transposed = sem("h0_transposed")
        h0T_copied = sem("h0T_copied")
        even_kept = sem("even_kept")
        odd_kept = sem("odd_kept")
        y1_multiplied = sem("y1_multiplied")
        y1_copied = sem("y1_copied")
        ring_in = [sem(f"ring_in{k}") for k in range(RING)]
        early_in = [sem(f"early_in{k}") for k in range(RING)]
        early_stage_ready = sem("early_stage_ready")
        early_done = sem("early_done")
        early_moved = sem("early_moved")
        early_added = sem("early_added")
        near_in = sem("near_in")
        diag_in = sem("diag_in")
        stage_ready = sem("stage_ready")
        tile_done = sem("tile_done")
        up_read = sem("up_read")
        low_read = sem("low_read")
        up_moved = sem("up_moved")
        low_moved = sem("low_moved")
        diag_moved = sem("diag_moved")
        cat_h = sem("cat_h")
        cat_m = sem("cat_m")
        gates_done = sem("gates_done")
        gates_ready = sem("gates_ready")
        rz_ready = sem("rz_ready")
        n_pre_ready = sem("n_pre_ready")
        n_ready = sem("n_ready")
        h_new_ready = sem("h_new_ready")
        hT_done = sem("hT_done")
        hT_ready = sem("hT_ready")
        h_kept = sem("h_kept")
        y2_done = sem("y2_done")
        y2_new_ready = sem("y2_new_ready")
        y2_ready = sem("y2_ready")
        diag_m2_done = sem("diag_m2_done")
        near_m2_done = sem("near_m2_done")
        diag_m2_moved = sem("diag_m2_moved")
        near_m2_moved = sem("near_m2_moved")
        held_read = sem("held_read")
        x_blk_in = sem("x_blk_in")
        out_ready = sem("out_ready")
        out_written = sem("out_written")
        dve_step = sem("dve_step")
        sp_passed = sem("sp_passed")
        pool_passed = sem("pool_passed")
        dve_passed = sem("dve_passed")

        from_one = {"pool": [h_kept], "pe": [gates_done], "dve": [early_done, up_read, low_read, held_read, y2_ready]}

        block = ctx.enter_context(nc.Block())

        def again_stage(q):
            return early_stage[:, 0] if q == RING - 1 else stage[:, q % STAGES, :, Y2]

        def chunks_of(row, odd):
            return row.rearrange("p (k o n) -> p k o n", o=2, n=P)[:, :, odd, :]

        def within(v, low, high):
            if isinstance(v, int):
                return v
            return nc.s_assert_within(v, low, high, skip_runtime_bounds_check_because="the branch taken bounds it")

        def since_lag(t):
            return within((t - LAG) & (NB - 1), 0, NB - 1 - LAG)

        @block.sync
        def _(sp):
            for k, (b0, b1) in enumerate(PIECES):
                sp.dma_start(h_tok[:, b0 * C:b1 * C, :], x[:, b0 * C:b1 * C, :]).then_inc(x_in[k], 16)
                if k == 1:
                    sp.dma_start(cst[:, :], consts).then_inc(consts_in, 16)
            for q in range(RING):
                sp.dma_start(ring[:, q], adj[0, q]).then_inc(ring_in[q], 16)

            def load_held(t):
                slot = sp.snap(t & 1)
                sp.wait_ge(held_read, t + 1)
                sp.sem_inc(sp_passed, 1)
                sp.dma_start(near[:, slot], adj[t, NB - 1]).then_inc(near_in, 16)
                sp.dma_start(diag[:, :, :], adj[t, NB - 2]).then_inc(diag_in, 16)

            with sp.Fori(0, NB) as t:
                with sp.If(t < LAG):
                    for n in range(FAR):
                        if n == RING:
                            load_held(t)
                        sp.wait_ge(tile_done, NB * t + n + 1)
                        sp.sem_inc(sp_passed, 1)
                        row = t if n < RING else sp.snap(within(t + 1, 1, LAG))
                        sp.dma_start(ring[:, n % RING], adj[row, (n + RING) % FAR]).then_inc(ring_in[n % RING], 16)
                with sp.Else():
                    early_row = sp.snap(since_lag(t))
                    for n in range(3 * RING):
                        if n == 2 * RING:
                            load_held(t)
                        if n < RING or (n - RING) % 2 == 0:
                            q = n if n < RING else RING + (n - RING) // 2
                            sp.wait_ge(tile_done, NB * t + q + 1)
                        else:
                            sp.wait_ge(early_done, EARLY * early_row + (n - RING) // 2 + 2)
                        sp.sem_inc(sp_passed, 1)
                        k = n % RING
                        if n < 2 * RING:
                            if n % 2 == 0:
                                sp.dma_start(ring[:, k], adj[t, RING + n // 2]).then_inc(ring_in[k], 16)
                            else:
                                sp.dma_start(ring[:, k], adj[early_row, n // 2]).then_inc(early_in[n // 2], 16)
                        else:
                            with sp.If(t < NB - 1):
                                sp.dma_start(ring[:, k], adj[within(t + 1, LAG, NB - 1), k]).then_inc(ring_in[k], 16)
                            with sp.Else():
                                sp.dma_start(ring[:, k], adj[0, EARLY + k]).then_inc(ring_in[k], 16)

            with sp.Fori(0, PAIRS) as j:
                for q in range(RING):
                    sp.wait_ge(tile_done, TILES + RING * j + q + 1)
                    sp.sem_inc(sp_passed, 1)
                    with sp.If(j < PAIRS - 1):
                        with sp.If(j > q - 1):
                            row_a = sp.snap(within(FAR - 1 - j, PAIRS, NB - 1))
                            sp.dma_start(ring[:, q], adj[row_a, q]).then_inc(ring_in[q], 16)
                        with sp.Else():
                            row_b = sp.snap(within(j + 1, 1, PAIRS - 1))
                            col = sp.snap(within(EARLY - 1 + q - j, 0, FAR - 1))
                            sp.dma_start(ring[:, q], adj[row_b, col]).then_inc(ring_in[q], 16)
                        sp.sem_inc(sp_passed, 1)
                    with sp.Else():
                        sp.dma_start(ring[:, q], adj[PAIRS, q]).then_inc(ring_in[q], 16)

        @block.gpsimd
        def _(pool):
            def stage_first(s, t, need):
                b = s % STAGES
                if s == NB - 2:
                    g, split = t + 1, NB - 1
                elif s == NB - 1:
                    g, split = t, None
                else:
                    g, split = t + 2 + s, NB - 2 - s
                if split is None or isinstance(t, int):
                    g = g if isinstance(g, int) else pool.snap(g)
                    need()
                    pool.tensor_copy(stage[:, b, :, Y1], y[:, g, :, Y1]).then_inc(stage_ready, 1)
                    return
                with pool.If(t < split):
                    gu = pool.snap(within(g, 0, NB - 1))
                    need()
                    pool.tensor_copy(stage[:, b, :, Y1], y[:, gu, :, Y1]).then_inc(stage_ready, 1)
                with pool.Else():
                    gl = pool.snap(within(g - NB, 0, NB - 1))
                    need()
                    pool.tensor_copy(stage[:, b, :, :], y[:, gl, :, :]).then_inc(stage_ready, 1)

            def stage_early(p, t):
                turn = pool.snap(since_lag(t))
                g = pool.snap(within(t - EARLY + p, 2, NB - 1))
                pool.wait_ge(early_done, EARLY * turn + max(p - STAGES + 1, 0) + 1)
                pool.sem_inc(pool_passed, 1)
                pool.tensor_copy(early_stage[:, p % STAGES, :, :], y[:, g, :, Y2]).then_inc(early_stage_ready, 1)

            def stage_again(q, j, least=0):
                to = again_stage(q)
                if q >= PAIRS - 1 or least > q or isinstance(j, int):
                    g = pool.snap(within(NB - j + q, LAG, NB - 1)) if least > q else q + LAG
                    pool.tensor_copy(to, y[:, g, :, Y2]).then_inc(stage_ready, 1)
                    return
                with pool.If(j > q):
                    g = pool.snap(within(NB - j + q, LAG, NB - 1))
                    pool.tensor_copy(to, y[:, g, :, Y2]).then_inc(stage_ready, 1)
                with pool.Else():
                    pool.tensor_copy(to, y[:, q + LAG, :, Y2]).then_inc(stage_ready, 1)

            def keep_h(row, count):
                at = pool.snap(row * C) if not isinstance(row, int) else row * C
                pool.wait_ge(hT_ready, count)
                pool.sem_inc(pool_passed, 1)
                pool.tensor_copy(chunks_of(feat[LO, row], 0), hT_pair[LO, 0])
                pool.tensor_copy(h_tok[:, bass.ds(at, C), :], h_new[:, :, :]).then_inc(h_kept, 1)

            def cat_hidden(row, count):
                pool.wait_ge(gates_done, count + 1)
                pool.sem_inc(pool_passed, 1)
                pool.tensor_copy(cat[LO, :], feat[LO, row]).then_inc(cat_h, 1)

            for s in from_one["pool"]:
                pool.sem_inc(s, 1)
            pool.memset(eps[:, :], EPS).then_inc(eps_set, 1)
            pool.memset(zeros[:, :], 0.0).then_inc(zeros_set, 1)
            for b in range(NB):
                pool.wait_ge(h0T_copied, b + 1)
                pool.tensor_copy(chunks_of(feat[LO, b], 0), hT_pair[LO, b % 2]).then_inc(even_kept, 1)
            pool.wait_ge(y1_copied, 2 * NB)
            for s in range(STAGES):
                stage_first(s, 0, lambda: None)
            with pool.Fori(0, NB) as t:
                for s in range(NB):
                    n = s + STAGES
                    done = pool.snap(NB * t + s + 1)

                    def need():
                        pool.wait_ge(tile_done, done)
                        pool.sem_inc(pool_passed, 1)

                    if n == FAR - 1:
                        pool.wait_ge(y2_ready, 2 * t + 1)
                        pool.sem_inc(pool_passed, 1)
                    if n < NB:
                        stage_first(n, t, need)
                    else:
                        with pool.If(t < NB - 1):
                            stage_first(n - NB, within(t + 1, 1, NB - 1), need)
                    if RING - 1 <= s < FAR - 1:
                        with pool.If(t >= LAG):
                            stage_early(s - (RING - 1), t)
                    if s == FAR - 4:
                        with pool.If(t >= 1):
                            keep_h(pool.snap(within(t - 1, 0, NB - 2)), t)
                    if s == FAR - 2:
                        cat_hidden(t, t)
            pool.wait_ge(tile_done, TILES)
            for q in range(STAGES):
                stage_again(q, 0)
            with pool.Fori(0, PAIRS) as j:
                for q in range(RING):
                    if q == RING - 1 - STAGES:
                        pool.wait_ge(y2_ready, 2 * NB + 1)
                    pool.wait_ge(tile_done, TILES + RING * j + q + 1)
                    pool.sem_inc(pool_passed, 1)
                    if q + STAGES < RING:
                        stage_again(q + STAGES, j)
                    else:
                        with pool.If(j < PAIRS - 1):
                            stage_again(q + STAGES - RING, within(j + 1, 1, PAIRS - 1), 1)
                        with pool.Else():
                            pool.tensor_copy(again_stage(q + STAGES - RING), y[:, LAG + q + STAGES - RING, :, Y2])\
                                .then_inc(stage_ready, 1)
                    if q == 1:
                        with pool.If(j >= 1):
                            cat_hidden(pool.snap(within(j - 1, 0, PAIRS - 1)), NB + 2 * j)
                    if q == 4:
                        with pool.If(j < 1):
                            keep_h(NB - 1, NB)
                            pool.wait_ge(h_kept, NB + 1)
                            cat_hidden(NB - 1, NB)
                    if q == RING - 1:
                        cat_hidden(pool.snap(within(FAR - j, PAIRS, FAR)), NB + 1 + 2 * j)
            first = TILES + RING * PAIRS
            for q in range(STAGES, RING):
                pool.wait_ge(tile_done, first + q - STAGES + 1)
                pool.tensor_copy(again_stage(q), y[:, PAIRS + 2 + q, :, Y2]).then_inc(stage_ready, 1)
                if q == STAGES:
                    cat_hidden(PAIRS - 1, NB + 2 * PAIRS)
            cat_hidden(PAIRS, NB + 1 + 2 * PAIRS)

        @block.tensor
        def _(pe):
            def halves(acc, st, cols, tile, first=False):
                for c in range(C):
                    half = (LO, HI)[c % 2]
                    last = pe.matmul(acc[half, :], st[:, c, cols], tile[:, c, :], start=first and c < 2, stop=True,
                                     skip_group_check=True)
                return last

            def full(acc, st, tile):
                for c in range(C):
                    last = pe.matmul(acc[:, :], st[:, c, :], tile[:, c, :], start=False, stop=True,
                                     skip_group_check=True)
                return last

            def clear(acc):
                pe.matmul(acc[:, :], zeros[:, 0:P], zeros[:, :], start=True, stop=True)

            def gate_products(layer, count):
                pe.wait_ge(cat_h, count)
                pe.wait_ge(cat_m, count)
                for c in range(C):
                    last = pe.matmul(g_ps[:, c, :], cat[:, c * P:(c + 1) * P], cst[:, WG[layer]], start=True,
                                     stop=True)
                last.then_inc(gates_done, 1)

            def transposes(bank, pairs):
                for k in range(C // 2):
                    last = pe.transpose(t_part(bank)[:, k, :], pairs(k), cst[:, IDENT])
                return last

            def y_products(t_bank, y_bank, hT, w):
                for k in range(C // 2):
                    for rows, to in zip((LO, HI), y_parts(t_bank, y_bank)):
                        last = pe.matmul(to[:, k, :], hT[rows, k, :], cst[rows, w], start=True, stop=True)
                return last

            def transpose_h(count):
                pe.wait_ge(h_new_ready, count)
                transposes(t_ps, lambda k: h_new[:, 2 * k:2 * k + 2, :].rearrange("p c d -> p (c d)"))\
                    .then_inc(hT_done, 1)

            def new_y2(count):
                pe.wait_ge(hT_ready, count)
                y_products(t_ps, y_ps, hT_pair[:, 0], W[1]).then_inc(y2_done, 1)

            def held_diag(count):
                pe.wait_ge(y2_new_ready, 2 * count)
                halves(acc_b, y2_new, slice(0, D), diag, first=True).then_inc(diag_m2_done, 1)

            def held_near(parity):
                halves(acc_a, y2_new, slice(0, D), near[:, parity], first=True).then_inc(near_m2_done, 1)

            for s in from_one["pe"]:
                pe.sem_inc(s, 1)
            pe.wait_ge(consts_in, 16)
            def transpose_h0(b):
                piece = [b0 for b0, _ in PIECES if b0 <= b]
                pe.wait_ge(h0_ready, len(piece))
                at = b * C
                transposes(t_banks[b % 3], lambda k: h_tok[:, at + 2 * k:at + 2 * k + 2, :].rearrange("p c d -> p (c d)"))\
                    .then_inc(h0_transposed, 1)

            transpose_h0(0)
            transpose_h0(1)
            for b in range(NB):
                pe.wait_ge(h0T_copied, b + 1)
                y_products(t_banks[b % 3], y_banks[b % 3], hT_pair[:, b % 2], W[0]).then_inc(y1_multiplied, 1)
                if b + 2 < NB:
                    if b >= 1:
                        pe.wait_ge(y1_copied, 2 * b)
                    transpose_h0(b + 2)
            pe.wait_ge(zeros_set, 1)
            pe.wait_ge(y1_copied, 2 * NB)

            def held_work(q, t, parity, layer_count):
                if q == 0:
                    gate_products(0, layer_count)
                elif q == 4:
                    transpose_h(layer_count)
                elif q == 5:
                    new_y2(layer_count)
                elif q == 6:
                    held_diag(layer_count)

            with pe.Fori(0, NB // 2) as u:
                for parity in range(2):
                    t = pe.snap(2 * u + parity)
                    pe.wait_ge(up_read, t + 1)
                    clear(acc_up)
                    pe.wait_ge(low_read, t + 1)
                    clear(acc_low)
                    def far_tile(q, k, uses, uppers=True):
                        st, slot = stage[:, q % STAGES], ring[:, k]
                        pe.wait_ge(stage_ready, NB * t + q + 1)
                        pe.wait_ge(ring_in[k], 16 * uses)
                        if not uppers:
                            full(acc_low, st, slot).then_inc(tile_done, 1)
                            return
                        with pe.If(t < NB - 2 - q):
                            halves(acc_up, st, Y1, slot).then_inc(tile_done, 1)
                        with pe.Else():
                            full(acc_low, st, slot).then_inc(tile_done, 1)

                    for q in range(RING):
                        far_tile(q, q, 2 * t + 1)
                        if q in (0, 4, 5, 6):
                            if parity:
                                held_work(q, t, parity, t)
                            else:
                                with pe.If(u >= 1):
                                    held_work(q, t, parity, t)
                        if q == 6:
                            with pe.If(u >= 1):
                                held_near(parity)
                    with pe.If(t < LAG):
                        for q in range(RING, FAR):
                            far_tile(q, q - RING, 2 * t + 2)
                    with pe.Else():
                        turn = pe.snap(since_lag(t))
                        for m in range(2 * RING):
                            k = m % RING
                            if m % 2 == 0:
                                far_tile(RING + m // 2, k, 2 * t + 2, uppers=False)
                            else:
                                pe.wait_ge(early_stage_ready, EARLY * turn + m // 2 + 1)
                                pe.wait_ge(early_in[m // 2], 16 * turn + 16)
                                halves(acc_early, early_stage[:, (m // 2) % STAGES], slice(0, D), ring[:, k],
                                       first=m == 1).then_inc(early_done, 1)
                    pe.wait_ge(stage_ready, NB * t + NB - 1)
                    pe.wait_ge(near_in, 16 * t + 16)
                    with pe.If(t < NB - 1):
                        halves(acc_up, stage[:, 0], Y1, near[:, parity]).then_inc(tile_done, 1)
                    with pe.Else():
                        full(acc_low, stage[:, 0], near[:, parity]).then_inc(tile_done, 1)
                    pe.wait_ge(stage_ready, NB * t + NB)
                    pe.wait_ge(diag_in, 16 * t + 16)
                    pe.wait_ge(held_read, t + 1)
                    halves(acc_a, stage[:, 1], Y1, diag, first=True).then_inc(tile_done, 1)
            def again_tile(q, acc, count, uses):
                pe.wait_ge(stage_ready, count)
                pe.wait_ge(ring_in[q], 16 * uses)
                halves(acc, again_stage(q), slice(0, D), ring[:, q]).then_inc(tile_done, 1)

            with pe.Fori(0, PAIRS) as j:
                for acc, free in ((acc_up, up_read), (acc_low, low_read)):
                    pe.wait_ge(free, NB + j + 1)
                    clear(acc)
                for q in range(RING):
                    count, uses = TILES + RING * j + q + 1, 2 * NB + 1 + j
                    if q == RING - 1:
                        again_tile(q, acc_up, count, uses)
                    else:
                        with pe.If(j > q):
                            again_tile(q, acc_low, count, uses)
                        with pe.Else():
                            again_tile(q, acc_up, count, uses)
                    if q == 0:
                        with pe.If(j >= 1):
                            gate_products(1, NB + 2 * j)
                        with pe.Else():
                            gate_products(0, NB)
                    if q == 2:
                        with pe.If(j < 1):
                            transpose_h(NB)
                    if q == 3:
                        with pe.If(j >= 1):
                            gate_products(1, NB + 1 + 2 * j)
                        with pe.Else():
                            new_y2(NB)
                            held_diag(NB)
                            held_near(0)
                    if q == RING - 1:
                        with pe.If(j < 1):
                            gate_products(1, NB + 1)
            pe.wait_ge(up_read, NB + PAIRS + 1)
            clear(acc_up)
            for q in range(RING):
                again_tile(q, acc_up, TILES + RING * PAIRS + q + 1, 2 * NB + 1 + PAIRS)
                if q == 0:
                    gate_products(1, NB + 2 * PAIRS)
                if q == 3:
                    gate_products(1, NB + 1 + 2 * PAIRS)
            gate_products(1, NB + 2 + 2 * PAIRS)

        @block.scalar
        def _(act):
            def copy_h0T(b):
                act.wait_ge(h0_transposed, b + 1)
                if b >= 2:
                    act.wait_ge(even_kept, b - 1)
                    act.wait_ge(odd_kept, b - 1)
                act.activation(hT_pair[:, b % 2], t_part(t_banks[b % 3]), ACT.Copy).then_inc(h0T_copied, 1)

            def copy_y1(b):
                act.wait_ge(y1_multiplied, b + 1)
                for odd, part in enumerate(y_parts(t_banks[b % 3], y_banks[b % 3])):
                    act.activation(y[:, b, odd::2, Y1], part, ACT.Copy).then_inc(y1_copied, 1)

            act.wait_ge(eps_set, 1)
            for k, (b0, b1) in enumerate(PIECES):
                part, sq = slice(b0 * C, b1 * C), ln_sq[k % 2]
                act.wait_ge(x_centred, k + 1)
                act.activation(sq[:, 0:(b1 - b0) * C, :], h_tok[:, part, :], ACT.Square).then_inc(x_squared, 1)
                act.wait_ge(squares_summed, k + 1)
                act.activation(ln_stat[:, 2, part], ln_stat[:, 2, part], ACT.Sqrt, bias=eps[:, :], scale=1.0 / D)\
                    .then_inc(std_ready, 1)
                if k >= 1:
                    for b in range(*PIECES[k - 1]):
                        copy_h0T(b)
                        if b >= 1:
                            copy_y1(b - 1)
            for b in range(*PIECES[-1]):
                copy_h0T(b)
                copy_y1(b - 1)
            copy_y1(NB - 1)

            def gate_functions(count):
                act.wait_ge(gates_ready, count)
                act.activation(rz[:, :, :], gates[:, :, 0:2 * D], ACT.Sigmoid).then_inc(rz_ready, 1)
                act.wait_ge(n_pre_ready, count)
                act.activation(n_gate[:, :, :], n_pre[:, :, :], ACT.Tanh).then_inc(n_ready, 1)

            with act.Fori(0, NB) as t:
                with act.If(t >= LAG):
                    act.wait_ge(early_done, EARLY * act.snap(since_lag(t)) + EARLY + 1)
                    act.activation(m_early_up[HI, :], acc_early[LO, :], ACT.Copy).then_inc(early_moved, 1)
                act.wait_ge(tile_done, NB * t + NB - 1)
                act.activation(m_up[HI, :], acc_up[LO, :], ACT.Copy).then_inc(up_moved, 1)
                act.activation(feat[HI, t], acc_low[LO, :], ACT.Copy).then_inc(low_moved, 1)
                act.wait_ge(tile_done, NB * t + NB)
                act.activation(m_diag_up[HI, :], acc_a[LO, :], ACT.Copy).then_inc(diag_moved, 1)
                gate_functions(t + 1)
                act.wait_ge(h_kept, t + 1)
                act.wait_ge(hT_done, t + 1)
                act.activation(hT_pair[:, 0], t_part(t_ps), ACT.Copy).then_inc(hT_ready, 1)
                act.wait_ge(diag_m2_done, t + 1)
                act.activation(m_up[HI, :], acc_b[LO, :], ACT.Copy).then_inc(diag_m2_moved, 1)
                with act.If(t >= 1):
                    act.wait_ge(near_m2_done, t)
                    act.activation(m_diag_up[HI, :], acc_a[LO, :], ACT.Copy).then_inc(near_m2_moved, 1)

            def finish_row(row, count, order):
                at = row * C if isinstance(row, int) else act.snap(row * C)
                act.dma_start(x_blk[:, :, :], x[:, bass.ds(at, C), :]).then_inc(x_blk_in, 16)
                gate_functions(count)
                act.wait_ge(out_ready, order + 1)
                act.dma_start(out[:, bass.ds(at, C), :], h_new[:, :, :]).then_inc(out_written, 16)

            act.wait_ge(held_read, NB + 1)
            finish_row(NB - 1, NB + 1, 0)
            with act.Fori(0, PAIRS) as j:
                act.wait_ge(tile_done, TILES + RING * j + RING)
                act.activation(m_up[HI, :], acc_low[LO, :], ACT.Copy).then_inc(low_moved, 1)
                act.activation(m_diag_up[HI, :], acc_up[LO, :], ACT.Copy).then_inc(up_moved, 1)
                finish_row(act.snap(within(FAR - j, PAIRS, FAR)), NB + 2 + 2 * j, 2 * j + 1)
                finish_row(j, NB + 3 + 2 * j, 2 * j + 2)
            act.wait_ge(tile_done, TILES + RING * PAIRS + RING)
            act.activation(m_diag_up[HI, :], acc_up[LO, :], ACT.Copy).then_inc(up_moved, 1)
            finish_row(PAIRS, NB + 2 + 2 * PAIRS, 2 * PAIRS + 1)
            act.wait_ge(out_written, 16 * NB)

        @block.vector
        def _(dve):
            class Chain:
                n = 0

            def step(ins):
                Chain.n += 1
                ins.then_inc(dve_step, 1)
                dve.wait_ge(dve_step, Chain.n)

            def new_chain():
                Chain.n = 0
                dve.sem_clear(dve_step)

            for s in from_one["dve"]:
                dve.sem_inc(s, 1)
            def keep_odd(b):
                dve.wait_ge(h0T_copied, b + 1)
                dve.tensor_copy(chunks_of(feat[LO, b], 1), hT_pair[HI, b % 2]).then_inc(odd_kept, 1)

            for k, (b0, b1) in enumerate(PIECES):
                n, rows = (b1 - b0) * C, slice(b0 * C, b1 * C)
                part = h_tok[:, rows, :]
                mean, rstd, var = (ln_stat[:, r, rows] for r in range(3))
                dve.wait_ge(x_in[k], 16)
                step(dve.tensor_reduce(mean, part, AX.X, ALU.add))
                step(dve.tensor_scalar(mean, mean, 1.0 / D, None, ALU.mult))
                dve.tensor_tensor(part, part, mean.unsqueeze(2).to_broadcast([P, n, D]), ALU.subtract)\
                    .then_inc(x_centred, 1)
                if k >= 2:
                    for b in range(*PIECES[k - 2]):
                        keep_odd(b)
                dve.wait_ge(x_squared, k + 1)
                dve.tensor_reduce(var, ln_sq[k % 2][:, 0:n, :], AX.X, ALU.add).then_inc(squares_summed, 1)
                dve.wait_ge(std_ready, k + 1)
                step(dve.reciprocal(rstd, var))
                dve.scalar_tensor_tensor(out=part, in0=part, scalar=0.0,
                                         in1=rstd.unsqueeze(2).to_broadcast([P, n, D]),
                                         op0=ALU.max, op1=ALU.mult).then_inc(h0_ready, 1)
            for piece in PIECES[-2:]:
                for b in range(*piece):
                    keep_odd(b)
            dve.wait_ge(consts_in, 16)
            for layer in range(2):
                rz_bias = cst[:, BIAS[layer].start:BIAS[layer].start + 2 * D]
                step(dve.tensor_tensor(rz_bias, rz_bias, cst[:, BHH[layer]], ALU.add))

            def new_state(layer, row, count):
                at = row * C if isinstance(row, int) else dve.snap(row * C)
                h = h_tok[:, bass.ds(at, C), :]
                dve.wait_ge(gates_done, count + 1)
                dve.tensor_tensor(gates[:, :, :], g_ps[:, :, :],
                                  cst[:, BIAS[layer]].unsqueeze(1).to_broadcast([P, C, 256]), ALU.add)\
                    .then_inc(gates_ready, 1)
                dve.wait_ge(rz_ready, count)
                step(dve.tensor_tensor(n_pre[:, :, :], rz[:, :, 0:D], gates[:, :, 3 * D:4 * D], ALU.mult))
                dve.tensor_tensor(n_pre[:, :, :], n_pre[:, :, :], gates[:, :, 2 * D:3 * D], ALU.add)\
                    .then_inc(n_pre_ready, 1)
                dve.wait_ge(n_ready, count)
                step(dve.tensor_tensor(h_mix[:, :, :], h, n_gate[:, :, :], ALU.subtract))
                step(dve.tensor_tensor(h_mix[:, :, :], h_mix[:, :, :], rz[:, :, D:2 * D], ALU.mult))
                step(dve.tensor_tensor(h_mix[:, :, :], h_mix[:, :, :], n_gate[:, :, :], ALU.add))

            def add_held(acc, up, moved, count, row):
                dve.wait_ge(moved, count)
                step(dve.tensor_tensor(m_sum[HI, :], acc[HI, :], up[HI, :], ALU.add))
                return dve.tensor_tensor(feat[HI, row], m_sum[HI, :], feat[HI, row], ALU.add)

            with dve.Fori(0, NB) as t:
                new_chain()
                with dve.If(t >= LAG):
                    early_row = dve.snap(since_lag(t))
                    dve.wait_ge(early_moved, early_row + 1)
                    dve.tensor_tensor(m_early_up[HI, :], acc_early[HI, :], m_early_up[HI, :], ALU.add)\
                        .then_inc(early_added, 1)
                    dve.wait_ge(early_added, 2 * early_row + 1)
                    dve.sem_inc(dve_passed, 1)
                    dve.tensor_tensor(feat[HI, early_row], m_early_up[HI, :], feat[HI, early_row], ALU.add)\
                        .then_inc(early_added, 1)
                dve.wait_ge(up_moved, t + 1)
                ins = dve.tensor_tensor(m_sum[HI, :], acc_up[HI, :], m_up[HI, :], ALU.add)
                ins.then_inc(up_read, 1)
                dve.wait_ge(up_read, t + 2)
                dve.wait_ge(low_moved, t + 1)
                ins = dve.tensor_tensor(m_sum[HI, :], acc_low[HI, :], m_sum[HI, :], ALU.add)
                ins.then_inc(low_read, 1)
                dve.wait_ge(low_read, t + 2)
                dve.wait_ge(diag_moved, t + 1)
                step(dve.tensor_tensor(m_sum[HI, :], acc_a[HI, :], m_sum[HI, :], ALU.add))
                dve.wait_ge(gates_done, t + 1)
                dve.tensor_tensor(cat[HI, :], m_sum[HI, :], m_diag_up[HI, :], ALU.add).then_inc(cat_m, 1)
                new_state(0, t, t + 1)
                dve.wait_ge(h_kept, t + 1)
                dve.tensor_scalar(h_new[:, :, :], h_mix[:, :, :], 0.0, None, ALU.max).then_inc(h_new_ready, 1)
                dve.wait_ge(y2_done, t + 1)
                for odd, part in enumerate(y_parts(t_ps, y_ps)):
                    dve.tensor_copy(y2_new[:, odd::2, :], part).then_inc(y2_new_ready, 1)
                step(dve.tensor_copy(chunks_of(feat[LO, t], 1), hT_pair[HI, 0]))
                for odd, part in enumerate(y_parts(t_ps, y_ps)):
                    dve.tensor_copy(y[:, t, odd::2, Y2], part).then_inc(y2_ready, 1)
                step(add_held(acc_b, m_up, diag_m2_moved, t + 1, t))
                with dve.If(t >= 1):
                    add_held(acc_a, m_diag_up, near_m2_moved, t, dve.snap(within(t - 1, 0, NB - 2)))\
                        .then_inc(held_read, 1)
                with dve.Else():
                    dve.sem_inc(held_read, 1)
                dve.wait_ge(held_read, t + 2)

            def finish_row(row, count, order):
                dve.wait_ge(cat_m, count)
                new_state(1, row, count)
                if not (isinstance(order, int) and order == 0):
                    dve.wait_ge(out_written, 16 * order)
                dve.wait_ge(x_blk_in, 16 * order + 16)
                ins = dve.scalar_tensor_tensor(out=h_new[:, :, :], in0=h_mix[:, :, :], scalar=0.0,
                                               in1=x_blk[:, :, :], op0=ALU.max, op1=ALU.add)
                ins.then_inc(out_ready, 1)

            new_chain()
            dve.tensor_copy(cat[HI, :], feat[HI, NB - 1]).then_inc(cat_m, 1)
            finish_row(NB - 1, NB + 1, 0)
            with dve.Fori(0, PAIRS) as j:
                new_chain()
                row_a = dve.snap(within(FAR - j, PAIRS, FAR))
                dve.wait_ge(low_moved, NB + 1 + j)
                dve.tensor_tensor(m_sum[HI, :], acc_low[HI, :], m_up[HI, :], ALU.add).then_inc(low_read, 1)
                dve.wait_ge(low_read, NB + 2 + j)
                dve.sem_inc(dve_passed, 1)
                dve.tensor_tensor(cat[HI, :], m_sum[HI, :], feat[HI, row_a], ALU.add).then_inc(cat_m, 1)
                dve.wait_ge(cat_m, NB + 2 + 2 * j)
                dve.wait_ge(up_moved, NB + 1 + j)
                dve.tensor_tensor(m_sum[HI, :], acc_up[HI, :], m_diag_up[HI, :], ALU.add).then_inc(up_read, 1)
                dve.wait_ge(up_read, NB + 2 + j)
                finish_row(row_a, NB + 2 + 2 * j, 2 * j + 1)
                dve.tensor_tensor(cat[HI, :], m_sum[HI, :], feat[HI, j], ALU.add).then_inc(cat_m, 1)
                finish_row(j, NB + 3 + 2 * j, 2 * j + 2)
            new_chain()
            dve.wait_ge(up_moved, NB + 1 + PAIRS)
            step(dve.tensor_tensor(m_sum[HI, :], acc_up[HI, :], m_diag_up[HI, :], ALU.add))
            dve.tensor_tensor(cat[HI, :], m_sum[HI, :], feat[HI, PAIRS], ALU.add).then_inc(cat_m, 1)
            finish_row(PAIRS, NB + 2 + 2 * PAIRS, 2 * PAIRS + 1)


def kernel(**inputs):
    import numpy as np
    import concourse.bacc as bacc
    from concourse.bass_utils import run_bass_kernel_spmd

    N, D, P, BLK = 8192, 64, 128, 512
    NB, C = N // BLK, BLK // P
    a = {k: np.asarray(v) for k, v in inputs.items()}

    adj = a["adj"].reshape(NB, BLK, NB, C, P)
    adj_tiles = np.empty((NB, NB, P, C, BLK), adj.dtype)
    for i in range(NB):
        order = [(i + 2 + s) % NB for s in range(NB)]
        adj_tiles[i] = adj[i][:, order].transpose(1, 3, 2, 0)
    x_tok = np.ascontiguousarray(a["x"].reshape(NB * C, P, D).transpose(1, 0, 2))

    consts = np.zeros((P, 1536), np.float32)
    for layer in range(2):
        name = "L0_gnn_%s" + str(layer + 1)
        whh, wih = a[name % "whh"].T, a[name % "wih"].T
        at = 256 * layer
        consts[0:D, at:at + 2 * D] = whh[:, 0:2 * D]
        consts[D:P, at:at + 2 * D] = wih[:, 0:2 * D]
        consts[D:P, at + 2 * D:at + 3 * D] = wih[:, 2 * D:]
        consts[0:D, at + 3 * D:at + 4 * D] = whh[:, 2 * D:]
        at = 512 + 256 * layer
        consts[:, at:at + 3 * D] = a[name % "bih"]
        consts[:, at + 3 * D:at + 4 * D] = a[name % "bhh"][2 * D:]
        consts[:, 1024 + 128 * layer:1024 + 128 * (layer + 1)] = a[name % "bhh"][0:2 * D]
        for half in (slice(0, D), slice(D, P)):
            consts[half, 1280 + D * layer:1280 + D * (layer + 1)] = a[name % "W"]
    consts[:, 1408:1536] = np.eye(P, dtype=np.float32)

    nc = bacc.Bacc("TRN2", target_bir_lowering=False, num_devices=1)
    arrays = {"adj_tiles": adj_tiles, "x_tok": x_tok, "consts": consts}
    args = [nc.dram_tensor(k, v.shape, mybir.dt.from_np(v.dtype), kind="ExternalInput").ap() for k, v in arrays.items()]
    args.append(nc.dram_tensor("out_tok", (P, NB * C, D), mybir.dt.float32, kind="ExternalOutput").ap())
    adjacency_gru_two_layers(nc, *args)
    got = run_bass_kernel_spmd(nc, [arrays], core_ids=[0]).results[0]["out_tok"]
    return np.ascontiguousarray(got.transpose(1, 0, 2)).reshape(N, D)
```

```python
import concourse.bass as bass
from concourse import mybir
from contextlib import ExitStack


def adjacency_gru_two_layers(nc: bass.Bass, adj: bass.AP, x: bass.AP, consts: bass.AP, out: bass.AP):
    fp32, bf16 = mybir.dt.float32, mybir.dt.bfloat16
    ALU, ACT, AX = mybir.AluOpType, mybir.ActivationFunctionType, mybir.AxisListType

    N, D = 8192, 64
    P = 128
    BLK = 512
    NB = N // BLK
    C = BLK // P
    FAR = NB - 2
    RING = FAR // 2
    STAGES = 2
    TILES = NB * NB
    EARLY = RING
    LAG = EARLY + 2
    TURNS = NB // 2
    HALVES = [range(0, C // 2), range(C // 2, C)]
    HALF = NB * C // 2
    PIECES = [(2, 3), (3, 5), (5, 8), (8, 12), (12, 16), (0, 2)]
    ORDER = [b for piece in PIECES for b in range(*piece)]
    EPS = 1e-5
    Y2, Y1 = slice(0, D), slice(D, 2 * D)
    LO, HI = slice(0, D), slice(D, 2 * D)
    WG = [slice(0, 256), slice(256, 512)]
    BIAS = [slice(512, 768), slice(768, 1024)]
    BHH = [slice(1024, 1152), slice(1152, 1280)]
    WW = [slice(1280, 1408), slice(1408, 1536)]
    IDENT = slice(1536, 1664)

    ctx = ExitStack()
    with ctx:
        def sb(name, shape, dt=fp32):
            return ctx.enter_context(nc.sbuf_tensor(name, shape, dt))

        def pb(name, shape):
            return ctx.enter_context(nc.psum_tensor(name, shape, fp32))

        def sem(name):
            return ctx.enter_context(nc.semaphore(name))

        cst = sb("cst", [P, IDENT.stop])
        eps = sb("eps", [P, 1])
        zeros = sb("zeros", [P, BLK], bf16)
        y = sb("y", [P, NB, C, 2 * D])
        feat = sb("feat", [P, NB, BLK])
        h_tok = sb("h_tok", [P, NB * C, D])
        ring = sb("ring", [P, RING, C, BLK])
        near = sb("near", [P, 2, C, BLK])
        diag = sb("diag", [P, C, BLK])
        stage = sb("stage", [P, STAGES, C, 2 * D])
        early_stage = sb("early_stage", [P, STAGES, C, D])
        m_early_up = sb("m_early_up", [P, BLK])
        cat = sb("cat", [P, BLK])
        m_sum = sb("m_sum", [P, BLK])
        m_up = sb("m_up", [P, BLK])
        m_diag_up = sb("m_diag_up", [P, BLK])
        gates = sb("gates", [P, C, 256])
        rz = sb("rz", [P, C, 2 * D])
        n_pre = sb("n_pre", [P, C, D])
        n_gate = sb("n_gate", [P, C, D])
        h_mix = sb("h_mix", [P, C, D])
        h_new = sb("h_new", [P, C, D])
        hT_pair = sb("hT_pair", [P, 2, C // 2, P])
        y2_new = sb("y2_new", [P, C, D])
        ln_stat = sb("ln_stat", [P, 3, NB * C])
        x_out = near.rearrange("p s c (k d) -> p (s c k) d", d=D)
        ln_sq = [near[:, 1, half:half + C // 2].rearrange("p c (k d) -> p (c k) d", d=D) for half in (0, C // 2)]

        acc_low = pb("acc_low", [P, BLK])
        acc_up = pb("acc_up", [P, BLK])
        acc_a = pb("acc_a", [P, BLK])
        acc_b = pb("acc_b", [P, BLK])
        g_ps = pb("g_ps", [P, C, 256])
        acc_early = g_ps[:, 0:2, :].rearrange("p c n -> p (c n)")
        t_ps = pb("t_ps", [P, BLK])
        y_ps = pb("y_ps", [P, BLK])

        def t_part(bank):
            return bank[:, 0:2 * P].rearrange("p (k n) -> p k n", n=P)

        def y_part(bank):
            return bank[:, 0:C * D].rearrange("p (c d) -> p c d", d=D)

        turn_banks = ((acc_low, acc_up), (acc_b, acc_a))

        t_banks = (t_ps, g_ps[:, 0:2, :].rearrange("p c n -> p (c n)"), acc_a)
        y_banks = (y_ps, g_ps[:, 2:4, :].rearrange("p c n -> p (c n)"), acc_b)

        consts_in = sem("consts_in")
        x_in = [sem(f"x_in{k}") for k in range(len(PIECES))]
        zeros_set = sem("zeros_set")
        eps_set = sem("eps_set")
        x_squared = sem("x_squared")
        x_centred = sem("x_centred")
        squares_summed = sem("squares_summed")
        std_ready = sem("std_ready")
        h0_ready = sem("h0_ready")
        h0_transposed = sem("h0_transposed")
        h0T_copied = sem("h0T_copied")
        even_kept = sem("even_kept")
        odd_kept = sem("odd_kept")
        y1_multiplied = sem("y1_multiplied")
        y1_copied = sem("y1_copied")
        ring_in = [sem(f"ring_in{k}") for k in range(RING)]
        early_in = [sem(f"early_in{k}") for k in range(RING)]
        early_stage_ready = sem("early_stage_ready")
        early_done = sem("early_done")
        early_moved = sem("early_moved")
        early_added = sem("early_added")
        near_in = sem("near_in")
        diag_in = sem("diag_in")
        stage_ready = sem("stage_ready")
        tile_done = sem("tile_done")
        up_read = sem("up_read")
        low_read = sem("low_read")
        up_moved = sem("up_moved")
        low_moved = sem("low_moved")
        diag_moved = sem("diag_moved")
        cat_h = sem("cat_h")
        cat_m = sem("cat_m")
        gates_done = sem("gates_done")
        gates_ready = sem("gates_ready")
        rz_ready = sem("rz_ready")
        n_pre_ready = sem("n_pre_ready")
        n_ready = sem("n_ready")
        h_new_ready = sem("h_new_ready")
        hT_done = sem("hT_done")
        hT_ready = sem("hT_ready")
        h_kept = sem("h_kept")
        y2_done = sem("y2_done")
        y2_new_ready = sem("y2_new_ready")
        y2_ready = sem("y2_ready")
        diag_m2_done = sem("diag_m2_done")
        near_m2_done = sem("near_m2_done")
        diag_m2_moved = sem("diag_m2_moved")
        near_m2_moved = sem("near_m2_moved")
        held_read = sem("held_read")
        high_x_in = sem("high_x_in")
        low_x_in = sem("low_x_in")
        out_ready = sem("out_ready")
        out_written = sem("out_written")
        dve_step = sem("dve_step")
        sp_passed = sem("sp_passed")
        pool_passed = sem("pool_passed")
        dve_passed = sem("dve_passed")

        from_one = {"pool": [h_kept], "pe": [gates_done], "dve": [early_done, up_read, low_read, held_read, y2_ready]}

        block = ctx.enter_context(nc.Block())

        def again_stage(q):
            return early_stage[:, 0] if q == RING - 1 else stage[:, q % STAGES, :, Y2]

        def chunks_of(row, odd):
            return row.rearrange("p (k o n) -> p k o n", o=2, n=P)[:, :, odd, :]

        def within(v, low, high):
            if isinstance(v, int):
                return v
            return nc.s_assert_within(v, low, high, skip_runtime_bounds_check_because="the branch taken bounds it")

        def since_lag(t):
            return within((t - LAG) & (NB - 1), 0, NB - 1 - LAG)

        @block.sync
        def _(sp):
            for k, (b0, b1) in enumerate(PIECES):
                sp.dma_start(h_tok[:, b0 * C:b1 * C, :], x[:, b0 * C:b1 * C, :]).then_inc(x_in[k], 16)
                if k == 1:
                    sp.dma_start(cst[:, :], consts).then_inc(consts_in, 16)
            for q in range(RING):
                sp.dma_start(ring[:, q], adj[0, q]).then_inc(ring_in[q], 16)

            def load_held(t):
                slot = sp.snap(t & 1)
                sp.wait_ge(held_read, t + 1)
                sp.sem_inc(sp_passed, 1)
                sp.dma_start(near[:, slot], adj[t, NB - 1]).then_inc(near_in, 16)
                sp.dma_start(diag[:, :, :], adj[t, NB - 2]).then_inc(diag_in, 16)

            with sp.Fori(0, NB) as t:
                with sp.If(t < LAG):
                    for n in range(FAR):
                        if n == RING:
                            load_held(t)
                        sp.wait_ge(tile_done, NB * t + n + 1)
                        sp.sem_inc(sp_passed, 1)
                        row = t if n < RING else sp.snap(within(t + 1, 1, LAG))
                        sp.dma_start(ring[:, n % RING], adj[row, (n + RING) % FAR]).then_inc(ring_in[n % RING], 16)
                with sp.Else():
                    early_row = sp.snap(since_lag(t))
                    for n in range(3 * RING):
                        if n == 2 * RING:
                            load_held(t)
                        if n < RING or (n - RING) % 2 == 0:
                            q = n if n < RING else RING + (n - RING) // 2
                            sp.wait_ge(tile_done, NB * t + q + 1)
                        else:
                            sp.wait_ge(early_done, EARLY * early_row + (n - RING) // 2 + 2)
                        sp.sem_inc(sp_passed, 1)
                        k = n % RING
                        if n < 2 * RING:
                            if n % 2 == 0:
                                sp.dma_start(ring[:, k], adj[t, RING + n // 2]).then_inc(ring_in[k], 16)
                            else:
                                sp.dma_start(ring[:, k], adj[early_row, n // 2]).then_inc(early_in[n // 2], 16)
                        else:
                            with sp.If(t < NB - 1):
                                sp.dma_start(ring[:, k], adj[within(t + 1, LAG, NB - 1), k]).then_inc(ring_in[k], 16)
                            with sp.Else():
                                sp.dma_start(ring[:, k], adj[0, EARLY + k]).then_inc(ring_in[k], 16)

            with sp.Fori(0, TURNS - 1) as j:
                for q in range(RING):
                    sp.wait_ge(tile_done, TILES + RING * j + q + 1)
                    sp.sem_inc(sp_passed, 1)
                    with sp.If(j < 1):
                        if q == 0:
                            sp.dma_start(x_out[:, HALF:, :], x[:, HALF:, :]).then_inc(high_x_in, 16)
                        if q == 4:
                            sp.dma_start(x_out[:, :HALF, :], x[:, :HALF, :]).then_inc(low_x_in, 16)
                    with sp.If(j > q - 1):
                        row_a = sp.snap(within(FAR - 1 - j, TURNS - 1, NB - 1))
                        sp.dma_start(ring[:, q], adj[row_a, q]).then_inc(ring_in[q], 16)
                    with sp.Else():
                        row_b = sp.snap(within(j + 1, 1, TURNS - 2))
                        col = sp.snap(within(RING - 1 + q - j, 0, FAR - 1))
                        sp.dma_start(ring[:, q], adj[row_b, col]).then_inc(ring_in[q], 16)

        @block.gpsimd
        def _(pool):
            def stage_first(s, t, done):
                b = s % STAGES
                if s == NB - 2:
                    g, split = t + 1, NB - 1
                elif s == NB - 1:
                    g, split = t, NB
                else:
                    g, split = t + 2 + s, NB - 2 - s

                def need():
                    pool.wait_ge(tile_done, done)
                    pool.sem_inc(pool_passed, 1)

                def y1():
                    gu = pool.snap(within(g, 0, NB - 1))
                    need()
                    pool.tensor_copy(stage[:, b, :, Y1], y[:, gu, :, Y1]).then_inc(stage_ready, 1)

                def both():
                    gl = pool.snap(within(g - NB, 0, NB - 1))
                    need()
                    pool.tensor_copy(stage[:, b, :, :], y[:, gl, :, :]).then_inc(stage_ready, 1)

                if split == NB:
                    y1()
                elif split == 1:
                    both()
                else:
                    with pool.If(t < split):
                        y1()
                    with pool.Else():
                        both()

            def stage_early(p, t):
                turn = pool.snap(since_lag(t))
                g = pool.snap(within(t - EARLY + p, 2, NB - 1))
                pool.wait_ge(early_done, EARLY * turn + max(p - STAGES + 1, 0) + 1)
                pool.sem_inc(pool_passed, 1)
                pool.tensor_copy(early_stage[:, p % STAGES, :, :], y[:, g, :, Y2]).then_inc(early_stage_ready, 1)

            def stage_again(q, j):
                with pool.If(j > q):
                    g = pool.snap(within(NB - j + q, LAG, NB - 1))
                    pool.tensor_copy(again_stage(q), y[:, g, :, Y2]).then_inc(stage_ready, 1)
                with pool.Else():
                    pool.tensor_copy(again_stage(q), y[:, q + LAG, :, Y2]).then_inc(stage_ready, 1)

            def keep_h(row, count):
                at = pool.snap(row * C) if not isinstance(row, int) else row * C
                pool.wait_ge(hT_ready, count)
                pool.sem_inc(pool_passed, 1)
                pool.tensor_copy(chunks_of(feat[LO, row], 0), hT_pair[LO, 0])
                pool.tensor_copy(h_tok[:, bass.ds(at, C), :], h_new[:, :, :]).then_inc(h_kept, 1)

            def cat_hidden(row, count):
                pool.wait_ge(gates_done, count + 1)
                pool.sem_inc(pool_passed, 1)
                pool.tensor_copy(cat[LO, :], feat[LO, row]).then_inc(cat_h, 1)

            for s in from_one["pool"]:
                pool.sem_inc(s, 1)
            pool.memset(eps[:, :], EPS).then_inc(eps_set, 1)
            pool.memset(zeros[:, :], 0.0).then_inc(zeros_set, 1)
            for i, b in enumerate(ORDER):
                pool.wait_ge(h0T_copied, i + 1)
                pool.tensor_copy(chunks_of(feat[LO, b], 0), hT_pair[LO, i % 2]).then_inc(even_kept, 1)
            pool.wait_ge(y1_copied, NB)
            pool.sem_inc(stage_ready, FAR)
            for b in range(STAGES):
                pool.tensor_copy(stage[:, b, :, Y1], y[:, 1 - b, :, Y1]).then_inc(stage_ready, 1)
            pool.wait_ge(even_kept, NB)
            pool.wait_ge(odd_kept, NB)
            cat_hidden(0, 0)
            for b in range(STAGES):
                pool.wait_ge(tile_done, FAR + b + 1)
                pool.tensor_copy(stage[:, b, :, Y1], y[:, 3 + b, :, Y1]).then_inc(stage_ready, 1)
            with pool.Fori(1, NB) as t:
                for s in range(NB):
                    n = s + STAGES
                    done = pool.snap(NB * t + s + 1)
                    if n == FAR - 1:
                        pool.wait_ge(y2_ready, t + 1)
                        pool.sem_inc(pool_passed, 1)
                    if n < NB:
                        stage_first(n, t, done)
                    else:
                        with pool.If(t < NB - 1):
                            stage_first(n - NB, within(t + 1, 1, NB - 1), done)
                    if RING - 1 <= s < FAR - 1:
                        with pool.If(t >= LAG):
                            stage_early(s - (RING - 1), t)
                    if s == FAR - 4:
                        keep_h(pool.snap(within(t - 1, 0, NB - 2)), t)
                    if s == FAR - 2:
                        cat_hidden(t, t)
            pool.wait_ge(tile_done, TILES)
            for q in range(STAGES):
                pool.tensor_copy(again_stage(q), y[:, q + LAG, :, Y2]).then_inc(stage_ready, 1)
            with pool.Fori(0, TURNS) as j:
                for q in range(RING):
                    if q == RING - 1 - STAGES:
                        pool.wait_ge(y2_ready, NB + 1)
                    pool.wait_ge(tile_done, TILES + RING * j + q + 1)
                    pool.sem_inc(pool_passed, 1)
                    if q + STAGES < RING:
                        stage_again(q + STAGES, j)
                    else:
                        with pool.If(j < TURNS - 1):
                            stage_again(q + STAGES - RING, within(j + 1, 1, TURNS - 1))
                    if q == 2:
                        with pool.If(j >= 1):
                            cat_hidden(pool.snap(within(j - 1, 0, TURNS - 2)), NB + 2 * j)
                    if q == 4:
                        with pool.If(j < 1):
                            keep_h(NB - 1, NB)
                            pool.wait_ge(h_kept, NB + 1)
                            cat_hidden(NB - 1, NB)
                    if q == RING - 2:
                        cat_hidden(pool.snap(within(FAR - j, TURNS - 1, FAR)), NB + 1 + 2 * j)

        @block.tensor
        def _(pe):
            def halves(acc, st, cols, tile, first=False):
                for c in range(C):
                    half = (LO, HI)[c % 2]
                    last = pe.matmul(acc[half, :], st[:, c, cols], tile[:, c, :], start=first and c < 2, stop=True,
                                     skip_group_check=True)
                return last

            def full(acc, st, tile):
                for c in range(C):
                    last = pe.matmul(acc[:, :], st[:, c, :], tile[:, c, :], start=False, stop=True,
                                     skip_group_check=True)
                return last

            def clear(acc):
                pe.matmul(acc[:, :], zeros[:, 0:P], zeros[:, :], start=True, stop=True)

            def gate_products(layer, count, chunks=range(C)):
                if chunks is not HALVES[1]:
                    pe.wait_ge(cat_h, count)
                pe.wait_ge(cat_m, count)
                for c in chunks:
                    last = pe.matmul(g_ps[:, c, :], cat[:, c * P:(c + 1) * P], cst[:, WG[layer]], start=True,
                                     stop=True)
                last.then_inc(gates_done, 1)

            def transposes(bank, pairs):
                for k in range(C // 2):
                    last = pe.transpose(t_part(bank)[:, k, :], pairs(k), cst[:, IDENT])
                return last

            def y_products(y_bank, hT, w):
                for k in range(C // 2):
                    last = pe.matmul(y_bank[:, 2 * k * D:2 * (k + 1) * D], hT[:, k, :], cst[:, w], start=True,
                                     stop=True)
                return last

            def transpose_h(count):
                pe.wait_ge(h_new_ready, count)
                transposes(t_ps, lambda k: h_new[:, 2 * k:2 * k + 2, :].rearrange("p c d -> p (c d)"))\
                    .then_inc(hT_done, 1)

            def new_y2(count):
                pe.wait_ge(hT_ready, count)
                y_products(y_ps, hT_pair[:, 0], WW[1]).then_inc(y2_done, 1)

            def held_diag(count):
                pe.wait_ge(y2_new_ready, count)
                halves(acc_b, y2_new, slice(0, D), diag, first=True).then_inc(diag_m2_done, 1)

            def held_near(parity):
                halves(acc_a, y2_new, slice(0, D), near[:, parity], first=True).then_inc(near_m2_done, 1)

            for s in from_one["pe"]:
                pe.sem_inc(s, 1)
            def transpose_h0(i):
                b = ORDER[i]
                pe.wait_ge(h0_ready, 1 + [b0 <= b < b1 for b0, b1 in PIECES].index(True))
                transposes(t_banks[i % 3],
                           lambda k: h_tok[:, b * C + 2 * k:b * C + 2 * k + 2, :].rearrange("p c d -> p (c d)"))\
                    .then_inc(h0_transposed, 1)

            pe.wait_ge(zeros_set, 1)
            clear(acc_up)
            clear(acc_low)
            pe.wait_ge(consts_in, 16)
            transpose_h0(0)
            transpose_h0(1)
            for i in range(NB):
                pe.wait_ge(h0T_copied, i + 1)
                y_products(y_banks[i % 3], hT_pair[:, i % 2], WW[0]).then_inc(y1_multiplied, 1)
                if i >= 1:
                    pe.wait_ge(y1_copied, i)
                if i + 2 < NB:
                    transpose_h0(i + 2)
                if 1 <= i <= FAR:
                    q = i - 1
                    pe.wait_ge(ring_in[q % RING], 16 * (q // RING + 1))
                    halves(acc_up, y[:, ORDER[q]], Y1, ring[:, q % RING]).then_inc(tile_done, 1)
            pe.wait_ge(y1_copied, NB)

            with pe.Fori(0, NB // 2) as u:
                for parity in range(2):
                    t = pe.snap(2 * u + parity)
                    def far_tile(q, k, uses, uppers=True):
                        st, slot = stage[:, q % STAGES], ring[:, k]
                        pe.wait_ge(stage_ready, NB * t + q + 1)
                        pe.wait_ge(ring_in[k], 16 * uses)
                        if not uppers:
                            full(acc_low, st, slot).then_inc(tile_done, 1)
                            return
                        with pe.If(t < NB - 2 - q):
                            halves(acc_up, st, Y1, slot).then_inc(tile_done, 1)
                        with pe.Else():
                            full(acc_low, st, slot).then_inc(tile_done, 1)

                    def far_tiles():
                        pe.wait_ge(up_read, t + 1)
                        clear(acc_up)
                        pe.wait_ge(low_read, t + 1)
                        clear(acc_low)
                        for q in range(RING):
                            far_tile(q, q, 2 * t + 1)
                            if q == 0:
                                gate_products(0, t)
                            elif q == 4:
                                transpose_h(t)
                            elif q == 5:
                                new_y2(t)
                            elif q == 6:
                                held_diag(t)
                                with pe.If(u >= 1):
                                    held_near(parity)
                        with pe.If(t < LAG):
                            for q in range(RING, FAR):
                                far_tile(q, q - RING, 2 * t + 2)
                        with pe.Else():
                            turn = pe.snap(since_lag(t))
                            for m in range(2 * RING):
                                k = m % RING
                                if m % 2 == 0:
                                    far_tile(RING + m // 2, k, 2 * t + 2, uppers=False)
                                else:
                                    pe.wait_ge(early_stage_ready, EARLY * turn + m // 2 + 1)
                                    pe.wait_ge(early_in[m // 2], 16 * turn + 16)
                                    halves(acc_early, early_stage[:, (m // 2) % STAGES], slice(0, D), ring[:, k],
                                           first=m == 1).then_inc(early_done, 1)

                    if parity:
                        far_tiles()
                    else:
                        with pe.If(u >= 1):
                            far_tiles()
                    pe.wait_ge(stage_ready, NB * t + NB - 1)
                    pe.wait_ge(near_in, 16 * t + 16)
                    with pe.If(t < NB - 1):
                        halves(acc_up, stage[:, 0], Y1, near[:, parity]).then_inc(tile_done, 1)
                    with pe.Else():
                        full(acc_low, stage[:, 0], near[:, parity]).then_inc(tile_done, 1)
                    pe.wait_ge(stage_ready, NB * t + NB)
                    pe.wait_ge(diag_in, 16 * t + 16)
                    pe.wait_ge(held_read, t + 1)
                    halves(acc_a, stage[:, 1], Y1, diag, first=True).then_inc(tile_done, 1)
            pe.wait_ge(up_read, NB + 1)
            clear(acc_up)
            pe.wait_ge(low_read, NB + 1)
            clear(acc_low)
            with pe.Fori(0, TURNS // 2) as u:
                for parity in range(2):
                    j = pe.snap(2 * u + parity)
                    bank_a, bank_b = turn_banks[parity]
                    for q in range(RING):
                        pe.wait_ge(stage_ready, TILES + RING * j + q + 1)
                        pe.wait_ge(ring_in[q], 16 * (2 * NB + 1 + j))
                        with pe.If(j > q):
                            halves(bank_a, again_stage(q), slice(0, D), ring[:, q]).then_inc(tile_done, 1)
                        with pe.Else():
                            halves(bank_b, again_stage(q), slice(0, D), ring[:, q]).then_inc(tile_done, 1)
                        if q in (1, 4):
                            if parity:
                                gate_products(1, NB + 2 * j + (q == 4))
                            else:
                                with pe.If(u >= 1):
                                    gate_products(1, NB + 2 * j + (q == 4))
                        if parity == 0:
                            with pe.If(u < 1):
                                if q == 0:
                                    gate_products(0, NB)
                                if q == 2:
                                    transpose_h(NB)
                                if q == 3:
                                    new_y2(NB)
                                    held_diag(NB)
                                    held_near(0)
                                if q == RING - 1:
                                    gate_products(1, NB + 1)
                        if q == RING - 2:
                            pe.wait_ge(held_read, NB + 1)
                            pe.wait_ge(low_read, NB + j + 1)
                            clear(turn_banks[1 - parity][0])
                            pe.wait_ge(up_read, NB + j + 1)
                            clear(turn_banks[1 - parity][1])
            for half in range(2):
                gate_products(1, NB + 2 * TURNS + half, HALVES[half])

        @block.scalar
        def _(act):
            def copy_h0T(i):
                act.wait_ge(h0_transposed, i + 1)
                if i >= 2:
                    act.wait_ge(even_kept, i - 1)
                    act.wait_ge(odd_kept, i - 1)
                act.activation(hT_pair[:, i % 2], t_part(t_banks[i % 3]), ACT.Copy).then_inc(h0T_copied, 1)

            def copy_y1(i):
                act.wait_ge(y1_multiplied, i + 1)
                act.activation(y[:, ORDER[i], :, Y1], y_part(y_banks[i % 3]), ACT.Copy).then_inc(y1_copied, 1)

            act.wait_ge(eps_set, 1)
            copied = 0
            for k in range(len(PIECES) + 1):
                if k < len(PIECES):
                    b0, b1 = PIECES[k]
                    part, sq = slice(b0 * C, b1 * C), ln_sq[k % 2]
                    act.wait_ge(x_centred, k + 1)
                    act.activation(sq[:, 0:(b1 - b0) * C, :], h_tok[:, part, :], ACT.Square).then_inc(x_squared, 1)
                    act.wait_ge(squares_summed, k + 1)
                    act.activation(ln_stat[:, 2, part], ln_stat[:, 2, part], ACT.Sqrt, bias=eps[:, :], scale=1.0 / D)\
                        .then_inc(std_ready, 1)
                if k >= 1:
                    for _ in range(*PIECES[k - 1]):
                        copy_h0T(copied)
                        if copied >= 1:
                            copy_y1(copied - 1)
                        copied += 1
            copy_y1(NB - 1)

            def gate_functions(count):
                act.wait_ge(gates_ready, count)
                act.activation(rz[:, :, :], gates[:, :, 0:2 * D], ACT.Sigmoid).then_inc(rz_ready, 1)
                act.wait_ge(n_pre_ready, count)
                act.activation(n_gate[:, :, :], n_pre[:, :, :], ACT.Tanh).then_inc(n_ready, 1)

            with act.Fori(0, NB) as t:
                with act.If(t >= LAG):
                    act.wait_ge(early_done, EARLY * act.snap(since_lag(t)) + EARLY + 1)
                    act.activation(m_early_up[HI, :], acc_early[LO, :], ACT.Copy).then_inc(early_moved, 1)
                act.wait_ge(tile_done, NB * t + NB - 1)
                act.activation(m_up[HI, :], acc_up[LO, :], ACT.Copy).then_inc(up_moved, 1)
                act.activation(feat[HI, t], acc_low[LO, :], ACT.Copy).then_inc(low_moved, 1)
                act.wait_ge(tile_done, NB * t + NB)
                act.activation(m_diag_up[HI, :], acc_a[LO, :], ACT.Copy).then_inc(diag_moved, 1)
                gate_functions(t + 1)
                act.wait_ge(h_kept, t + 1)
                act.wait_ge(hT_done, t + 1)
                act.activation(hT_pair[:, 0], t_part(t_ps), ACT.Copy).then_inc(hT_ready, 1)
                act.wait_ge(diag_m2_done, t + 1)
                act.activation(m_up[HI, :], acc_b[LO, :], ACT.Copy).then_inc(diag_m2_moved, 1)
                with act.If(t >= 1):
                    act.wait_ge(near_m2_done, t)
                    act.activation(m_diag_up[HI, :], acc_a[LO, :], ACT.Copy).then_inc(near_m2_moved, 1)

            def finish_row(row, count, order):
                at = row * C if isinstance(row, int) else act.snap(row * C)
                gate_functions(count)
                act.wait_ge(out_ready, order + 1)
                act.dma_start(out[:, bass.ds(at, C), :], x_out[:, bass.ds(at, C), :]).then_inc(out_written, 16)

            act.wait_ge(held_read, NB + 1)
            finish_row(NB - 1, NB + 1, 0)
            with act.Fori(0, TURNS // 2) as u:
                for parity in range(2):
                    j = act.snap(2 * u + parity)
                    bank_a, bank_b = turn_banks[parity]

                    def finish_turn():
                        act.wait_ge(tile_done, TILES + RING * j + RING)
                        act.activation(m_up[HI, :], bank_a[LO, :], ACT.Copy).then_inc(low_moved, 1)
                        act.activation(m_diag_up[HI, :], bank_b[LO, :], ACT.Copy).then_inc(up_moved, 1)
                        finish_row(act.snap(within(FAR - j, TURNS, FAR)), NB + 2 + 2 * j, 2 * j + 1)
                        finish_row(j, NB + 3 + 2 * j, 2 * j + 2)

                    if parity:
                        with act.If(u < TURNS // 2 - 1):
                            finish_turn()
                    else:
                        finish_turn()
            count, row = NB + 2 * TURNS, TURNS - 1
            act.wait_ge(tile_done, TILES + RING * TURNS)
            for chunks in HALVES:
                part = slice(chunks.start * P, chunks.stop * P)
                act.activation(m_up[HI, part], turn_banks[1][0][LO, part], ACT.Copy).then_inc(low_moved, 1)
            for half, chunks in enumerate(HALVES):
                part = slice(chunks.start, chunks.stop)
                act.wait_ge(gates_ready, count + half)
                act.activation(rz[:, part, :], gates[:, part, 0:2 * D], ACT.Sigmoid).then_inc(rz_ready, 1)
            for half, chunks in enumerate(HALVES):
                part = slice(chunks.start, chunks.stop)
                act.wait_ge(n_pre_ready, count + half)
                act.activation(n_gate[:, part, :], n_pre[:, part, :], ACT.Tanh).then_inc(n_ready, 1)
            for half, chunks in enumerate(HALVES):
                part = slice(row * C + chunks.start, row * C + chunks.stop)
                act.wait_ge(out_ready, NB + half)
                act.dma_start(out[:, part, :], x_out[:, part, :]).then_inc(out_written, 16)
            act.wait_ge(out_written, 16 * (NB + 1))

        @block.vector
        def _(dve):
            class Chain:
                n = 0

            def step(ins):
                Chain.n += 1
                ins.then_inc(dve_step, 1)
                dve.wait_ge(dve_step, Chain.n)

            def new_chain():
                Chain.n = 0
                dve.sem_clear(dve_step)

            for s in from_one["dve"]:
                dve.sem_inc(s, 1)
            def keep_odd(piece):
                for b in range(*piece):
                    i = ORDER.index(b)
                    dve.wait_ge(h0T_copied, i + 1)
                    dve.tensor_copy(chunks_of(feat[LO, b], 1), hT_pair[HI, i % 2]).then_inc(odd_kept, 1)

            for k, (b0, b1) in enumerate(PIECES):
                n, rows = (b1 - b0) * C, slice(b0 * C, b1 * C)
                part = h_tok[:, rows, :]
                mean, rstd, var = (ln_stat[:, r, rows] for r in range(3))
                dve.wait_ge(x_in[k], 16)
                step(dve.tensor_reduce(mean, part, AX.X, ALU.add))
                step(dve.tensor_scalar(mean, mean, 1.0 / D, None, ALU.mult))
                dve.tensor_tensor(part, part, mean.unsqueeze(2).to_broadcast([P, n, D]), ALU.subtract)\
                    .then_inc(x_centred, 1)
                if k >= 2:
                    keep_odd(PIECES[k - 2])
                dve.wait_ge(x_squared, k + 1)
                dve.tensor_reduce(var, ln_sq[k % 2][:, 0:n, :], AX.X, ALU.add).then_inc(squares_summed, 1)
                dve.wait_ge(std_ready, k + 1)
                step(dve.reciprocal(rstd, var))
                dve.scalar_tensor_tensor(out=part, in0=part, scalar=0.0,
                                         in1=rstd.unsqueeze(2).to_broadcast([P, n, D]),
                                         op0=ALU.max, op1=ALU.mult).then_inc(h0_ready, 1)
            keep_odd(PIECES[-2])
            keep_odd(PIECES[-1])
            dve.wait_ge(consts_in, 16)
            for layer in range(2):
                rz_bias = cst[:, BIAS[layer].start:BIAS[layer].start + 2 * D]
                step(dve.tensor_tensor(rz_bias, rz_bias, cst[:, BHH[layer]], ALU.add))

            def new_state(layer, row, count):
                at = row * C if isinstance(row, int) else dve.snap(row * C)
                h = h_tok[:, bass.ds(at, C), :]
                dve.wait_ge(gates_done, count + 1)
                dve.tensor_tensor(gates[:, :, :], g_ps[:, :, :],
                                  cst[:, BIAS[layer]].unsqueeze(1).to_broadcast([P, C, 256]), ALU.add)\
                    .then_inc(gates_ready, 1)
                dve.wait_ge(rz_ready, count)
                step(dve.tensor_tensor(n_pre[:, :, :], rz[:, :, 0:D], gates[:, :, 3 * D:4 * D], ALU.mult))
                dve.tensor_tensor(n_pre[:, :, :], n_pre[:, :, :], gates[:, :, 2 * D:3 * D], ALU.add)\
                    .then_inc(n_pre_ready, 1)
                dve.wait_ge(n_ready, count)
                step(dve.tensor_tensor(h_mix[:, :, :], h, n_gate[:, :, :], ALU.subtract))
                step(dve.tensor_tensor(h_mix[:, :, :], h_mix[:, :, :], rz[:, :, D:2 * D], ALU.mult))
                step(dve.tensor_tensor(h_mix[:, :, :], h_mix[:, :, :], n_gate[:, :, :], ALU.add))

            def add_held(acc, up, moved, count, row):
                dve.wait_ge(moved, count)
                step(dve.tensor_tensor(m_sum[HI, :], acc[HI, :], up[HI, :], ALU.add))
                return dve.tensor_tensor(feat[HI, row], m_sum[HI, :], feat[HI, row], ALU.add)

            with dve.Fori(0, NB) as t:
                new_chain()
                with dve.If(t >= LAG):
                    early_row = dve.snap(since_lag(t))
                    dve.wait_ge(early_moved, early_row + 1)
                    dve.tensor_tensor(m_early_up[HI, :], acc_early[HI, :], m_early_up[HI, :], ALU.add)\
                        .then_inc(early_added, 1)
                    dve.wait_ge(early_added, 2 * early_row + 1)
                    dve.sem_inc(dve_passed, 1)
                    dve.tensor_tensor(feat[HI, early_row], m_early_up[HI, :], feat[HI, early_row], ALU.add)\
                        .then_inc(early_added, 1)
                dve.wait_ge(up_moved, t + 1)
                ins = dve.tensor_tensor(m_sum[HI, :], acc_up[HI, :], m_up[HI, :], ALU.add)
                ins.then_inc(up_read, 1)
                dve.wait_ge(up_read, t + 2)
                dve.wait_ge(low_moved, t + 1)
                ins = dve.tensor_tensor(m_sum[HI, :], acc_low[HI, :], m_sum[HI, :], ALU.add)
                ins.then_inc(low_read, 1)
                dve.wait_ge(low_read, t + 2)
                dve.wait_ge(diag_moved, t + 1)
                step(dve.tensor_tensor(m_sum[HI, :], acc_a[HI, :], m_sum[HI, :], ALU.add))
                dve.wait_ge(gates_done, t + 1)
                dve.tensor_tensor(cat[HI, :], m_sum[HI, :], m_diag_up[HI, :], ALU.add).then_inc(cat_m, 1)
                new_state(0, t, t + 1)
                dve.wait_ge(h_kept, t + 1)
                dve.tensor_scalar(h_new[:, :, :], h_mix[:, :, :], 0.0, None, ALU.max).then_inc(h_new_ready, 1)
                dve.wait_ge(y2_done, t + 1)
                dve.tensor_copy(y2_new[:, :, :], y_part(y_ps)).then_inc(y2_new_ready, 1)
                step(dve.tensor_copy(chunks_of(feat[LO, t], 1), hT_pair[HI, 0]))
                dve.tensor_copy(y[:, t, :, Y2], y_part(y_ps)).then_inc(y2_ready, 1)
                step(add_held(acc_b, m_up, diag_m2_moved, t + 1, t))
                with dve.If(t >= 1):
                    add_held(acc_a, m_diag_up, near_m2_moved, t, dve.snap(within(t - 1, 0, NB - 2)))\
                        .then_inc(held_read, 1)
                with dve.Else():
                    dve.sem_inc(held_read, 1)
                dve.wait_ge(held_read, t + 2)

            def finish_row(row, count):
                at = row * C if isinstance(row, int) else dve.snap(row * C)
                dve.wait_ge(cat_m, count)
                new_state(1, row, count)
                x_row = x_out[:, bass.ds(at, C), :]
                dve.wait_ge(high_x_in, 16)
                if not isinstance(row, int):
                    dve.wait_ge(low_x_in, 16)
                dve.scalar_tensor_tensor(out=x_row, in0=h_mix[:, :, :], scalar=0.0, in1=x_row, op0=ALU.max,
                                         op1=ALU.add).then_inc(out_ready, 1)

            new_chain()
            dve.tensor_copy(cat[HI, :], feat[HI, NB - 1]).then_inc(cat_m, 1)
            finish_row(NB - 1, NB + 1)
            with dve.Fori(0, TURNS // 2) as u:
                for parity in range(2):
                    new_chain()
                    j = dve.snap(2 * u + parity)
                    bank_a, bank_b = turn_banks[parity]

                    def finish_turn():
                        row_a = dve.snap(within(FAR - j, TURNS, FAR))
                        dve.wait_ge(low_moved, NB + 1 + j)
                        dve.tensor_tensor(m_sum[HI, :], bank_a[HI, :], m_up[HI, :], ALU.add).then_inc(low_read, 1)
                        dve.wait_ge(low_read, NB + 2 + j)
                        dve.sem_inc(dve_passed, 1)
                        dve.tensor_tensor(cat[HI, :], m_sum[HI, :], feat[HI, row_a], ALU.add).then_inc(cat_m, 1)
                        dve.wait_ge(cat_m, NB + 2 + 2 * j)
                        dve.wait_ge(up_moved, NB + 1 + j)
                        dve.tensor_tensor(m_sum[HI, :], bank_b[HI, :], m_diag_up[HI, :], ALU.add).then_inc(up_read, 1)
                        dve.wait_ge(up_read, NB + 2 + j)
                        finish_row(row_a, NB + 2 + 2 * j)
                        dve.tensor_tensor(cat[HI, :], m_sum[HI, :], feat[HI, j], ALU.add).then_inc(cat_m, 1)
                        finish_row(j, NB + 3 + 2 * j)

                    if parity:
                        with dve.If(u < TURNS // 2 - 1):
                            finish_turn()
                    else:
                        finish_turn()

            new_chain()
            count, row = NB + 2 * TURNS, TURNS - 1
            for half, chunks in enumerate(HALVES):
                part = slice(chunks.start * P, chunks.stop * P)
                dve.wait_ge(low_moved, NB + TURNS + half)
                step(dve.tensor_tensor(m_sum[HI, part], turn_banks[1][0][HI, part], m_up[HI, part], ALU.add))
                dve.tensor_tensor(cat[HI, part], m_sum[HI, part], feat[HI, row, part], ALU.add).then_inc(cat_m, 1)
            for half, chunks in enumerate(HALVES):
                part = slice(chunks.start, chunks.stop)
                dve.wait_ge(gates_done, count + half + 1)
                dve.tensor_tensor(gates[:, part, :], g_ps[:, part, :],
                                  cst[:, BIAS[1]].unsqueeze(1).to_broadcast([P, C // 2, 256]), ALU.add)\
                    .then_inc(gates_ready, 1)
            for half, chunks in enumerate(HALVES):
                part = slice(chunks.start, chunks.stop)
                dve.wait_ge(rz_ready, count + half)
                step(dve.tensor_tensor(n_pre[:, part, :], rz[:, part, 0:D], gates[:, part, 3 * D:4 * D], ALU.mult))
                dve.tensor_tensor(n_pre[:, part, :], n_pre[:, part, :], gates[:, part, 2 * D:3 * D], ALU.add)\
                    .then_inc(n_pre_ready, 1)
            for half, chunks in enumerate(HALVES):
                part, row_part = (slice(at + chunks.start, at + chunks.stop) for at in (0, row * C))
                mix = h_mix[:, part, :]
                dve.wait_ge(n_ready, count + half)
                step(dve.tensor_tensor(mix, h_tok[:, row_part, :], n_gate[:, part, :], ALU.subtract))
                step(dve.tensor_tensor(mix, mix, rz[:, part, D:2 * D], ALU.mult))
                step(dve.tensor_tensor(mix, mix, n_gate[:, part, :], ALU.add))
                dve.scalar_tensor_tensor(out=x_out[:, row_part, :], in0=mix, scalar=0.0, in1=x_out[:, row_part, :],
                                         op0=ALU.max, op1=ALU.add).then_inc(out_ready, 1)


def kernel(**inputs):
    import numpy as np
    import concourse.bacc as bacc
    from concourse.bass_utils import run_bass_kernel_spmd

    N, D, P, BLK = 8192, 64, 128, 512
    NB, C = N // BLK, BLK // P
    a = {k: np.asarray(v) for k, v in inputs.items()}

    adj = a["adj"].reshape(NB, BLK, NB, C, P)
    adj_tiles = np.empty((NB, NB, P, C, BLK), adj.dtype)
    for i in range(NB):
        order = [(i + 2 + s) % NB for s in range(NB)]
        adj_tiles[i] = adj[i][:, order].transpose(1, 3, 2, 0)
    x_tok = np.ascontiguousarray(a["x"].reshape(NB * C, P, D).transpose(1, 0, 2))

    consts = np.zeros((P, 1664), np.float32)
    for layer in range(2):
        name = "L0_gnn_%s" + str(layer + 1)
        whh, wih = a[name % "whh"].T, a[name % "wih"].T
        at = 256 * layer
        consts[0:D, at:at + 2 * D] = whh[:, 0:2 * D]
        consts[D:P, at:at + 2 * D] = wih[:, 0:2 * D]
        consts[D:P, at + 2 * D:at + 3 * D] = wih[:, 2 * D:]
        consts[0:D, at + 3 * D:at + 4 * D] = whh[:, 2 * D:]
        at = 512 + 256 * layer
        consts[:, at:at + 3 * D] = a[name % "bih"]
        consts[:, at + 3 * D:at + 4 * D] = a[name % "bhh"][2 * D:]
        consts[:, 1024 + 128 * layer:1024 + 128 * (layer + 1)] = a[name % "bhh"][0:2 * D]
        at = 1280 + 128 * layer
        consts[0:D, at:at + D] = consts[D:P, at + D:at + 2 * D] = a[name % "W"]
    consts[:, 1536:1664] = np.eye(P, dtype=np.float32)

    nc = bacc.Bacc("TRN2", target_bir_lowering=False, num_devices=1)
    arrays = {"adj_tiles": adj_tiles, "x_tok": x_tok, "consts": consts}
    args = [nc.dram_tensor(k, v.shape, mybir.dt.from_np(v.dtype), kind="ExternalInput").ap() for k, v in arrays.items()]
    args.append(nc.dram_tensor("out_tok", (P, NB * C, D), mybir.dt.float32, kind="ExternalOutput").ap())
    adjacency_gru_two_layers(nc, *args)
    got = run_bass_kernel_spmd(nc, [arrays], core_ids=[0]).results[0]["out_tok"]
    return np.ascontiguousarray(got.transpose(1, 0, 2)).reshape(N, D)
```
